# Optimizing a Trainium2 kernel written in Bass

```python
import numpy as np
import jax
import jax.numpy as jnp

def _softmax(x, axis=-1):
    return jax.nn.softmax(x, axis=axis)

def _gelu(x):
    return jax.nn.gelu(x, approximate=True)

def _silu(x):
    return jax.nn.silu(x)

def _sigmoid(x):
    return jax.nn.sigmoid(x)

def _layernorm(x, axis=-1, eps=1e-05):
    m = jnp.mean(x, axis=axis, keepdims=True)
    v = jnp.var(x, axis=axis, keepdims=True)
    return (x - m) / jnp.sqrt(v + eps)

def _scatter_add(tgt, idx, src, axis=0):
    return tgt.at[idx].add(src)

def _segment_sum(src, seg, n):
    return jax.ops.segment_sum(src, seg, n)
kernel_name = 'mk_adaln_ffn_d2_seqx_r4_6b55d6'

def setup_inputs(seed: int=0):
    np.random.seed(seed)
    _w = jnp.asarray

    def _rec_inputs():
        import jax
        import jax.numpy as jnp
        _rk = jax.random.key(seed)
        x = -0.000125 + 0.9999 * jax.random.normal(jax.random.fold_in(_rk, 1), (16, 256, 512), jnp.float32)
        _lenS = 256 - jax.random.randint(jax.random.fold_in(_rk, 7), (16,), 0, max(1, 256 // 4) + 1, jnp.int32)
        _lenS2 = 256 - jax.random.randint(jax.random.fold_in(_rk, 8), (16,), 0, max(1, 256 // 4) + 1, jnp.int32)
        cond_2048 = 7.82532e-05 + 0.0100527 * jax.random.normal(jax.random.fold_in(_rk, 11), (16, 512), jnp.float32)
        return (x, cond_2048)
    x, cond_2048 = _rec_inputs()

    def _L0_cond_setup():
        import jax, jax.numpy as jnp
        import numpy as np
        NUM_BLOCKS = 8
        NUM_LAYERS = 4
        EPS = 1e-06
        key = jax.random.key(seed)
        ks = jax.random.split(key, 6)
        B, S, H = (4, 1024, 512)
        inputs = jax.random.normal(ks[0], (B, S, H), dtype=jnp.float32)
        query_vectors = jax.random.normal(ks[1], (NUM_LAYERS, H), dtype=jnp.float32) * 0.01
        lim = float(np.sqrt(6.0 / (H + H)))
        Wk = jax.random.uniform(ks[2], (H, H), minval=-lim, maxval=lim, dtype=jnp.float32)
        Wo = jax.random.uniform(ks[3], (H, H), minval=-lim, maxval=lim, dtype=jnp.float32)
        rms_weight = jnp.ones((H,), dtype=jnp.float32)
        ln_gamma = jnp.ones((H,), dtype=jnp.float32)
        ln_beta = jnp.zeros((H,), dtype=jnp.float32)
        return {'inputs': inputs, 'layer_idx': 1, 'rms_weight': rms_weight, 'query_vectors': query_vectors, 'Wk': Wk, 'Wo': Wo, 'ln_gamma': ln_gamma, 'ln_beta': ln_beta}
    _L0_cond_all = _L0_cond_setup()
    _L0_cond_in = {k: v for k, v in _L0_cond_all.items() if k in ('rms_weight', 'Wk', 'Wo', 'ln_gamma', 'ln_beta')}
    del _L0_cond_all

    def _L0_ffn_setup():
        import jax, jax.numpy as jnp
        import numpy as np
        N_EMBD = 512
        D_FF = 4 * N_EMBD
        BATCH, SEQ = (4, 512)
        EPS = 1e-05

        def rmsnorm(x):
            return x * jax.lax.rsqrt(jnp.mean(x * x, axis=-1, keepdims=True) + 1e-06)

        def activation_quant(x):
            scale = 127.0 / jnp.clip(jnp.max(jnp.abs(x), axis=-1, keepdims=True), EPS, None)
            return jnp.clip(jnp.round(x * scale), -128, 127) / scale

        def weight_quant(w):
            scale = 1.0 / jnp.clip(jnp.mean(jnp.abs(w)), EPS, None)
            return jnp.clip(jnp.round(w * scale), -1, 1) / scale

        def bitlinear(x, w):
            xn = rmsnorm(x)
            xq = xn + jax.lax.stop_gradient(activation_quant(xn) - xn)
            wq = w + jax.lax.stop_gradient(weight_quant(w) - w)
            return jnp.einsum('bsi,oi->bso', xq, wq)
        key = jax.random.key(seed)
        k0, k1, k2, k3 = jax.random.split(key, 4)
        x = jax.random.normal(k0, (BATCH, SEQ, N_EMBD), dtype=jnp.float32)
        s_in = 1.0 / np.sqrt(N_EMBD)
        s_ff = 1.0 / np.sqrt(D_FF)
        w1 = jax.random.normal(k1, (D_FF, N_EMBD), dtype=jnp.float32) * s_in
        w2 = jax.random.normal(k2, (D_FF, N_EMBD), dtype=jnp.float32) * s_in
        w3 = jax.random.normal(k3, (N_EMBD, D_FF), dtype=jnp.float32) * s_ff
        return {'x': x, 'w1': w1, 'w2': w2, 'w3': w3}
    _L0_ffn_all = _L0_ffn_setup()
    _L0_ffn_in = {k: v for k, v in _L0_ffn_all.items() if k in ('w1', 'w2', 'w3')}
    del _L0_ffn_all

    def _L1_cond_setup():
        import jax, jax.numpy as jnp
        import numpy as np
        key = jax.random.key(seed)
        k1, k2 = jax.random.split(key)
        B, T, C, K = (4, 1024, 512, 4)
        x = jax.random.normal(k1, (B, T, C), dtype=jnp.float32)
        w = jax.random.normal(k2, (K, 1, C), dtype=jnp.float32) * 0.1
        return {'x': x, 'w': w}
    _L1_cond_all = _L1_cond_setup()
    _L1_cond_in = {k: v for k, v in _L1_cond_all.items() if k in ()}
    del _L1_cond_all

    def _L1_ffn_setup():
        import jax, jax.numpy as jnp
        import numpy as np
        K_TOP = 2
        key = jax.random.key(seed)
        k0, k1, k2 = jax.random.split(key, 3)
        B, S, D, E, F = (4, 512, 512, 8, 512)
        x = jax.random.normal(k0, (B, S, D), dtype=jnp.float32)
        Wr = jax.random.normal(k1, (D, E), dtype=jnp.float32) * 0.02
        We = jax.random.normal(k2, (E, D, F), dtype=jnp.float32) * 0.02
        be = jnp.zeros((E, F), dtype=jnp.float32)
        return {'x': x, 'Wr': Wr, 'We': We, 'be': be}
    _L1_ffn_all = _L1_ffn_setup()
    _L1_ffn_in = {k: v for k, v in _L1_ffn_all.items() if k in ('Wr', 'We', 'be')}
    del _L1_ffn_all
    return {'x': x, 'cond_2048': cond_2048, 'L0_cond_rms_weight': _L0_cond_in['rms_weight'], 'L0_cond_Wk': _L0_cond_in['Wk'], 'L0_cond_Wo': _L0_cond_in['Wo'], 'L0_cond_ln_gamma': _L0_cond_in['ln_gamma'], 'L0_cond_ln_beta': _L0_cond_in['ln_beta'], 'L0_ffn_w1': _L0_ffn_in['w1'], 'L0_ffn_w2': _L0_ffn_in['w2'], 'L0_ffn_w3': _L0_ffn_in['w3'], 'L1_ffn_Wr': _L1_ffn_in['Wr'], 'L1_ffn_We': _L1_ffn_in['We'], 'L1_ffn_be': _L1_ffn_in['be']}

def reference(x, cond_2048, L0_cond_rms_weight, L0_cond_Wk, L0_cond_Wo, L0_cond_ln_gamma, L0_cond_ln_beta, L0_ffn_w1, L0_ffn_w2, L0_ffn_w3, L1_ffn_Wr, L1_ffn_We, L1_ffn_be):
    import jax
    import jax.numpy as jnp

    def _L0_cond_ref(inputs, layer_idx, rms_weight, query_vectors, Wk, Wo, ln_gamma, ln_beta):
        import jax, jax.numpy as jnp
        import numpy as np
        NUM_BLOCKS = 8
        NUM_LAYERS = 4
        EPS = 1e-06
        B, S, H = inputs.shape
        block_size = max(1, S // NUM_BLOCKS)
        n_blocks = S // block_size
        block_repr = inputs.reshape(B, n_blocks, block_size, H).sum(axis=2)
        keys = jnp.einsum('bnh,kh->bnk', block_repr, Wk)
        rms = jnp.sqrt(jnp.mean(keys * keys, axis=-1, keepdims=True) + EPS)
        keys = keys / rms * rms_weight
        q = query_vectors[layer_idx]
        scores = jnp.einsum('bnh,h->bn', keys, q)
        attn = jax.nn.softmax(scores, axis=-1)
        attended = jnp.einsum('bn,bnh->bh', attn, block_repr)
        attended = jnp.broadcast_to(attended[:, None, :], (B, S, H))
        proj = jnp.einsum('bsh,kh->bsk', attended, Wo)
        x = inputs + proj
        mu = jnp.mean(x, axis=-1, keepdims=True)
        var = jnp.mean((x - mu) ** 2, axis=-1, keepdims=True)
        out = (x - mu) / jnp.sqrt(var + EPS) * ln_gamma + ln_beta
        return out

    def _L0_ffn_ref(x, w1, w2, w3):
        import jax, jax.numpy as jnp
        import numpy as np
        N_EMBD = 512
        D_FF = 4 * N_EMBD
        BATCH, SEQ = (4, 512)
        EPS = 1e-05

        def rmsnorm(x):
            return x * jax.lax.rsqrt(jnp.mean(x * x, axis=-1, keepdims=True) + 1e-06)

        def activation_quant(x):
            scale = 127.0 / jnp.clip(jnp.max(jnp.abs(x), axis=-1, keepdims=True), EPS, None)
            return jnp.clip(jnp.round(x * scale), -128, 127) / scale

        def weight_quant(w):
            scale = 1.0 / jnp.clip(jnp.mean(jnp.abs(w)), EPS, None)
            return jnp.clip(jnp.round(w * scale), -1, 1) / scale

        def bitlinear(x, w):
            xn = rmsnorm(x)
            xq = xn + jax.lax.stop_gradient(activation_quant(xn) - xn)
            wq = w + jax.lax.stop_gradient(weight_quant(w) - w)
            return jnp.einsum('bsi,oi->bso', xq, wq)
        h = jax.nn.silu(bitlinear(x, w1)) * bitlinear(x, w2)
        return bitlinear(h, w3)

    def _L1_cond_ref(x, w):
        import jax, jax.numpy as jnp
        import numpy as np
        K = w.shape[0]
        C = x.shape[-1]
        y = jax.lax.conv_general_dilated(x, w, window_strides=(1,), padding=[(K - 1, 0)], dimension_numbers=('NHC', 'HIO', 'NHC'), feature_group_count=C)
        return y

    def _L1_ffn_ref(x, Wr, We, be):
        import jax, jax.numpy as jnp
        import numpy as np
        K_TOP = 2
        logits = jnp.einsum('bsd,de->bse', x, Wr)
        w, sel = jax.lax.top_k(logits, K_TOP)
        w = jax.nn.softmax(w, axis=-1)
        E = We.shape[0]
        gate = jnp.einsum('bsk,bske->bse', w, jax.nn.one_hot(sel, E, dtype=w.dtype))
        out = jnp.zeros(x.shape[:2] + (We.shape[2],), dtype=x.dtype)
        for e in range(E):
            out = out + gate[..., e:e + 1] * (jnp.einsum('bsd,df->bsf', x, We[e]) + be[e])
        return out
    x = x + _L0_ffn_ref(_L0_cond_ref(x, 1, L0_cond_rms_weight, cond_2048, L0_cond_Wk, L0_cond_Wo, L0_cond_ln_gamma, L0_cond_ln_beta), L0_ffn_w1, L0_ffn_w2, L0_ffn_w3)
    x = x + _L1_ffn_ref(_L1_cond_ref(x, cond_2048[:, None, :]), L1_ffn_Wr, L1_ffn_We, L1_ffn_be)
    return x

_drawn_inputs = setup_inputs


def setup_inputs(seed=0):
    import zlib

    import numpy as np

    out = dict(_drawn_inputs(seed))
    spreads = {'L0_cond_rms_weight': (1.0, 0.2),
     'L0_cond_ln_gamma': (1.0, 0.2),
     'L0_cond_ln_beta': (0.0, 0.1),
     'L1_ffn_be': (0.0, 0.1)}
    factors = {'L1_ffn_We': 4.453}
    for name, (base, spread) in spreads.items():
        noise = np.random.default_rng([zlib.crc32(name.encode()), seed]).standard_normal(out[name].shape)
        drawn = base * np.exp(spread * noise) if base else spread * noise
        out[name] = jnp.asarray(drawn.astype(out[name].dtype))
    for name, factor in factors.items():
        out[name] = (out[name] * factor).astype(out[name].dtype)
    return out
```

```python
from contextlib import ExitStack

import concourse.bass as bass
from concourse import mybir

F32 = mybir.dt.float32
F32R = mybir.dt.float32r
BF16 = mybir.dt.bfloat16
I16 = mybir.dt.int16
I32 = mybir.dt.int32
ALU = mybir.AluOpType
ACT = mybir.ActivationFunctionType
AX = mybir.AxisListType

P = 128
QD = 32
NQ = P // QD
QMAX = 127.0
CLIP = 1e-5
RMS_EPS = 1e-6


def adaln_ffn_moe(nc, x, cond, taps, rms_w, WkT, WoT, gamma, beta, w1T, w2T, w3T, Wr, We, be, out):
    B, S, D = x.shape
    FF = w1T.shape[1]
    E = We.shape[0]
    K = taps.shape[1]
    TOK = B * S
    NT = TOK // P
    TB = S // P
    BLK = 8
    NBLK = B * BLK
    KD = D // P
    KF = FF // P
    CH = 512
    NC = FF // CH
    NI = D // NQ
    GI = 16
    NG = NI // GI
    WIN = 2 * QD
    PADW = 3 * QD
    WCOUNT = float(D * FF)
    assert S // BLK == QD and TB == 2 and KD == NQ and NBLK == P and K <= QD and D == CH

    ctx = ExitStack()
    with ctx:
        def sem(name):
            return ctx.enter_context(nc.semaphore(name))

        def dram(name, shape):
            return nc.dram_tensor(name, shape, F32, kind="Internal").ap()

        proj_d = dram("proj_scratch", (B, D))
        taps_d = dram("taps_scratch", (D, PADW))
        x1_d = dram("x1_scratch", (TOK, D))
        z_d = dram("z_scratch", (TOK, D))

        base = (nc.sbuf_base + 31) // 32 * 32
        words = (nc.sbuf_usable_end - base) // 4

        def place(name, at, shape, dt=F32):
            n = 4 if dt in (F32, F32R) else 2
            size = n
            for s in shape[1:]:
                size *= s
            assert at >= 0 and at + size // 4 <= words, (name, at, size, words)
            return nc.alloc_sbuf_tensor_at(name, list(shape), dt, offset=base + 4 * at)

        a_x, a_w12, a_w3, a_T = 0, NT * D, NT * D + KD * FF, NT * D + KD * FF + KF * D // 2
        a_h = a_T + NI * WIN
        X = place("X", a_x, [P, NT, D])
        XP = place("XP", a_x, [P, NBLK, NI])
        W12 = place("W12", a_w12, [P, KD, 2 * FF], BF16)
        W3 = place("W3", a_w3, [P, KF, D], BF16)
        T = place("T", a_T, [P, NI, WIN])
        stage0 = place("stage0", a_T, [P, 4, FF])
        stage1 = place("stage1", a_h, [P, 4, FF])
        H = [place(f"H{i}", a_h + FF * i, [P, FF]) for i in range(2)]
        a = a_h + 2 * FF
        QT = place("QT", a, [P, KF, P], BF16)
        Qh = place("Qh", a + FF // 2, [P, FF], BF16)
        SG = [place(f"SG{i}", a + FF + CH * i, [P, CH]) for i in range(2)]
        Ih = place("Ih", a + FF + 2 * CH, [P, FF], I16)
        BD = [place(f"BD{i}", a_h + 2 * GI * P * i, [P, 2, GI, P]) for i in range(2)]
        a_s = a_h + 4 * FF
        assert a + FF + 2 * CH + FF // 2 <= a_s
        SUM = [place(f"SUM{i}", a_s + D * i, [P, D]) for i in range(2)]
        Y = [place(f"Y{i}", a_s + D * (2 + i), [P, D]) for i in range(2)]
        PJ = [place(f"PJ{i}", a_s + D * (4 + i), [P, D]) for i in range(2)]
        X1 = [place(f"X1{i}", a_s + D * (6 + i), [P, D]) for i in range(2)]
        WkS = place("WkS", a_s, [P, KD, D])
        WoS = place("WoS", a_s + KD * D, [P, KD, D])
        a = a_s + 8 * D
        Iy = place("Iy", a, [P, D], I16)
        Qy = [place(f"Qy{i}", a + D // 2 * (1 + i), [P, D], BF16) for i in range(2)]
        QyT = [place(f"QyT{i}", a + D // 2 * (3 + i), [P, KD, P], BF16) for i in range(2)]
        a += D // 2 * 5
        GAM = place("GAM", a, [P, D])
        BET = place("BET", a + D, [P, D])
        JUNK = place("JUNK", a + 2 * D, [P, FF], BF16)
        TMP = place("TMP", a + 2 * D, [P, FF], I16)
        a += 2 * D + FF // 2
        TZ = place("TZ", a, [P, KD, PADW])
        a += KD * PADW
        IDF = place("IDF", a, [P, P])
        IDB = place("IDB", a + P, [P, P], BF16)
        sm = place("sm", a + P + P // 2, [P, 96])
        R = place("R", a_w3, [P, D])
        RT = place("RT", a_w3 + D, [P, KD, P])
        RW = place("RW", a_w3 + 2 * D, [P, D])
        QB = place("QB", a_w3 + 3 * D, [P, D])
        PROJ = place("PROJ", a_w3 + 4 * D, [P, D])
        KJ = place("KJ", a_w3 + 5 * D, [P, D])
        SELW = place("SELW", a_w3 + 6 * D, [P, 2 * P - NQ])
        ONES = place("ONES", a_w3 + 6 * D + 2 * P, [P, P])
        ROWS = place("ROWS", a_w3 + 6 * D + 3 * P, [1, P])
        EROW = place("EROW", a_w3 + 7 * D, [1, 3 * P])
        MSK = place("MSK", a_w3 + 7 * D + 3 * P, [P, B])
        AMX = place("AMX", a_w3 + 7 * D + 3 * P + B, [P, B])
        ATT = place("ATT", a_w3 + 7 * D + 3 * P + 2 * B, [P, KD * B])
        DOT, KSS, KRS, SCO, ATC = (sm[:, 64 + i:65 + i] for i in range(5))
        GMX, GSM = sm[0:1, 70:70 + B], EROW[:, 2 * P:2 * P + B]

        def col(i):
            return [sm[:, 2 * i + t:2 * i + t + 1] for t in range(2)]

        YMS, YR, YM, YO, YI, YQ, OG, OU = (col(i) for i in range(8))
        HMS, HR, HM, HO, HI, HQ, OD, RSTD = (col(8 + i) for i in range(8))
        MV = [sm[:, 32 + 2 * t:34 + 2 * t] for t in range(2)]
        BS = [sm[:, 36 + 6 * t:42 + 6 * t] for t in range(2)]
        WSUM, WMEAN, WSC = ([sm[:, 48 + 3 * i + w:49 + 3 * i + w] for w in range(3)] for i in range(3))
        MHALF = sm[:, 57:58]
        WPART = place("WPART", a_w3 + 7 * D + 3 * P + 2 * B + KD * B, [P, 12])

        NEXP = KD * D
        WH = [place(f"WH{e}", 2 * e * NEXP, [P, KD, D], F32R) for e in range(E)]
        WL = [place(f"WL{e}", (2 * e + 1) * NEXP, [P, KD, D], F32R) for e in range(E)]
        a = 2 * E * NEXP
        assert a <= a_T + NI * WIN // 2 and a + 2 * NEXP <= a_h
        WST = [place(f"WST{i}", a + NEXP * i, [P, KD, D]) for i in range(2)]
        ZR = [place(f"ZR{i}", a_h + D * i, [P, D]) for i in range(2)]
        X1C = [place(f"X1C{i}", a_h + D * (2 + i), [P, D]) for i in range(2)]
        ZH = [place(f"ZH{i}", a_h + D * (4 + i), [P, KD, P], F32R) for i in range(2)]
        ZL = [place(f"ZL{i}", a_h + D * (6 + i), [P, KD, P], F32R) for i in range(2)]
        BEV = place("BEV", a_h + 8 * D, [2, E * D])
        a = a_s
        ZC = [place(f"ZC{i}", a + D * i, [P, NQ, NI]) for i in range(2)]
        ZT = [place(f"ZT{i}", a + D * (2 + i), [P, NQ, NI]) for i in range(2)]
        a += 4 * D
        BEP = place("BEP", a_s, [2, E * D], F32R)
        NR = NT * E
        LG, L2, OH1, OH2, CAND, IOE = (place(n, a_s + 8 * D + NR * i, [P, NT, E]) for i, n in
                                       enumerate(("LG", "L2", "OH1", "OH2", "CAND", "IOE")))
        a = a_s + 8 * D + 6 * NR
        GATE = place("GATE", a, [P, NR])
        a += NR
        M1, M2, S1, S2, EX, P1, P2 = (place(n, a + NT * i, [P, NT]) for i, n in
                                      enumerate(("M1", "M2", "S1", "S2", "EX", "P1", "P2")))
        WRS = place("WRS", a + 7 * NT, [P, KD, E])
        BMK = place("BMK", a + 7 * NT + KD * E, [2, 2])
        ONF = place("ONF", a + 7 * NT + KD * E + 8, [2, P])
        ONR = place("ONR", a + 7 * NT + KD * E + 8 + P, [2, P], F32R)

        PS = ctx.enter_context(nc.psum_tensor("PS", [P, 8, CH], F32))
        bank = [PS[:, i, :] for i in range(8)]
        GP, UP = [bank[0], bank[2]], [bank[1], bank[3]]
        TR = [bank[4].bitcast(BF16), bank[5].bitcast(BF16)]
        DN = bank[6]
        TY = bank[7].bitcast(BF16)

        x_in = [sem(f"x_in{i}") for i in range(8)]
        att_in, wo_in, norm_in, taps_in, taps_out = sem("att_in"), sem("wo_in"), sem("norm_in"), sem("taps_in"), sem("taps_out")
        w_in = [[sem(f"w_in{w}_{c}") for c in range(4)] for w in range(3)]
        T_in, proj_out = sem("T_in"), sem("proj_out")
        pj_in = [sem(f"pj_in{t}") for t in range(2)]
        x1_out = [sem(f"x1_out{t}") for t in range(2)]
        xp_in, z_out = sem("xp_in"), sem("z_out")
        const = sem("const")
        repr_sum, repr_ev, repr_T, repr_Tev, keys_done = sem("repr_sum"), sem("repr_ev"), sem("repr_T"), sem("repr_Tev"), sem("keys_done")
        rwq_done, kss_done, dot_done, krs_done = sem("rwq_done"), sem("kss_done"), sem("dot_done"), sem("krs_done")
        sco_done, row_done, soft_v, soft_e, colT_done = sem("sco_done"), sem("row_done"), sem("soft_v"), sem("soft_e"), sem("colT_done")
        att_v, att_pe, att_copy, proj_pe, proj_ev = sem("att_v"), sem("att_pe"), sem("att_copy"), sem("proj_pe"), sem("proj_ev")
        att_pool = sem("att_pool")
        w_abs, w_tot, w_step, w_round, w_tern = (sem(n) for n in ("w_abs", "w_tot", "w_step", "w_round", "w_tern"))
        sum_done, stats_done, mv_done, gam_done, y_done, ymax_done = (sem(n) for n in ("sum_done", "stats_done", "mv_done", "gam_done", "y_done", "ymax_done"))
        ysq_done, rstd_done, yo_done, yi_done, yq_done = (sem(n) for n in ("ysq_done", "rstd_done", "yo_done", "yi_done", "yq_done"))
        yint_done, yqt_done, tr1_done, qyt_done = (sem(n) for n in ("yint_done", "yqt_done", "tr1_done", "qyt_done"))
        pool_a = sem("pool_a")
        g_done, u_done, silu_done, hm_done = (sem(n) for n in ("g_done", "u_done", "silu_done", "hm_done"))
        hsq_done, hmax_done, ho_done, hi_done, hq_done = (sem(n) for n in ("hsq_done", "hmax_done", "ho_done", "hi_done", "hq_done"))
        pool_h = sem("pool_h")
        hint_done, qh_done, tr2_done, qt_done, down_done, x1_done = (sem(n) for n in ("hint_done", "qh_done", "tr2_done", "qt_done", "down_done", "x1_done"))
        bd_zero, bd_done, conv_done, z_done = sem("bd_zero"), sem("bd_done"), sem("conv_done"), sem("z_done")
        zc_done, zt_pe, zt_done, lg_done = sem("zc_done"), sem("zt_pe"), sem("zt_done"), sem("lg_done")
        route_in, route_v, route_e = sem("route_in"), sem("route_v"), sem("route_e")
        route_p = sem("route_p")
        we_in = [sem(f"we_in{i}") for i in range(2)]
        wh_done, wl_done, be_in, be_done, gate_done = sem("wh_done"), sem("wl_done"), sem("be_in"), sem("be_done"), sem("gate_done")
        zr_in = [sem(f"zr_in{t}") for t in range(2)]
        x1c_in = [sem(f"x1c_in{t}") for t in range(2)]
        out_done = [sem(f"out_done{t}") for t in range(2)]
        trz_done, zh_done, zl_done, exp_done, mix_done = (sem(n) for n in ("trz_done", "zh_done", "zl_done", "exp_done", "mix_done"))

        block = ctx.enter_context(nc.Block())

        def over_tiles(eng, slot):
            for n in range(2 * TB):
                slot(n, n % TB, n == 0, False)
            with eng.Fori(2, B - 1) as b:
                for t in range(TB):
                    slot(b * TB + t, t, False, False)
            for t in range(TB):
                slot(NT - TB + t, t, False, t == TB - 1)

        def early(n):
            return isinstance(n, int) and n < 2

        EORD = [4, 5, 6, 7, 0, 1, 2, 3]

        @block.sync
        def _(sp):
            sp.dma_start(RW[:], bass.AP(rms_w.tensor, 0, [[0, P], [1, D]])).then_inc(att_in, 16)
            sp.dma_start(QB[:], bass.AP(cond.tensor, D, [[0, P], [1, D]])).then_inc(att_in, 16)
            for i in range(8):
                w = NT // 8
                sp.dma_start(X[:, w * i:w * i + w, :], x.rearrange("b (u p) d -> p (b u) d", p=P)[:, w * i:w * i + w, :]) \
                    .then_inc(x_in[i], 16)
            sp.dma_start(GAM[:], bass.AP(gamma.tensor, 0, [[0, P], [1, D]])).then_inc(norm_in, 16)
            sp.dma_start(BET[:], bass.AP(beta.tensor, 0, [[0, P], [1, D]])).then_inc(norm_in, 16)
            sp.wait_ge(const, 8)
            sp.dma_start(TZ[:, :, WIN - K:WIN], taps.rearrange("(k p) u -> p k u", p=P)).then_inc(taps_in, 16)
            sp.wait_ge(taps_in, 16)
            sp.dma_start(taps_d.rearrange("(k p) u -> p k u", p=P), TZ[:]).then_inc(taps_out, 16)
            sp.wait_ge(w_tern, 4)
            for c in range(4):
                kc = KF // 4
                sp.dma_start(stage0[:, c, :], w3T.rearrange("(k p) d -> p k d", p=P)[:, kc * c:kc * c + kc, :]) \
                    .then_inc(w_in[2][c], 16)
            sp.wait_ge(proj_ev, 1)
            sp.dma_start(proj_d, PROJ[0:B, :]).then_inc(proj_out, 16)
            sp.wait_ge(proj_out, 16)

            def load_pj(n, t):
                if not early(n):
                    sp.wait_ge(sum_done, n - 1)
                b = n // TB if isinstance(n, int) else (n - t) // TB
                sp.dma_start(PJ[t][:], bass.AP(proj_d.tensor, b * D, [[0, P], [1, D]])).then_inc(pj_in[t], 16)

            def store_x1(n, t):
                sp.wait_ge(x1_done, n + 1)
                sp.dma_start(x1_d[bass.ds(n * P, P), :], X1[t][:]).then_inc(x1_out[t], 16)

            def load_xp(b):
                for t in range(TB):
                    sp.wait_ge(x1_out[t], 16 * b + 16)
                for j in range(NQ):
                    src = bass.AP(x1_d.tensor, b * S * D + j * NI, [[D, QD], [QD * D, BLK], [1, NI]])
                    sp.dma_start(XP[QD * j:QD * j + QD, bass.ds(b * BLK, BLK), :], src).then_inc(xp_in, 16)

            load_pj(0, 0)
            load_pj(1, 1)
            sp.wait_ge(w_tern, 12)
            sp.wait_ge(taps_out, 16)
            for j in range(NQ):
                src = bass.AP(taps_d.tensor, j * NI * PADW, [[1, QD], [PADW, NI], [1, WIN]])
                sp.dma_start(T[QD * j:QD * j + QD, :, :], src).then_inc(T_in, 16)
            for t in range(TB):
                load_pj(2 + t, t)
                if t:
                    store_x1(0, 0)
            with sp.Fori(1, B - 1) as b:
                load_pj(b * TB + 2, 0)
                store_x1(b * TB - 1, 1)
                load_xp(b - 1)
                load_pj(b * TB + 3, 1)
                store_x1(b * TB, 0)
            store_x1(NT - 3, 1)
            load_xp(B - 2)
            store_x1(NT - 2, 0)
            store_x1(NT - 1, 1)
            load_xp(B - 1)
            sp.dma_start(WRS[:], Wr.rearrange("(k p) e -> p k e", p=P)).then_inc(route_in, 16)
            sp.wait_ge(z_done, 4 * NG)
            with sp.Fori(0, B) as b:
                for j in range(NQ):
                    dst = bass.AP(z_d.tensor, b * S * D + j * NI, [[D, QD], [QD * D, BLK], [1, NI]])
                    sp.dma_start(dst, XP[QD * j:QD * j + QD, bass.ds(b * BLK, BLK), :]).then_inc(z_out, 16)
            sp.dma_start(BEV[:], bass.AP(be.tensor, 0, [[0, 2], [1, E * D]])).then_inc(be_in, 16)
            for i, e in enumerate(EORD):
                if i >= 2:
                    sp.wait_ge(wl_done, i - 1)
                sp.dma_start(WST[i % 2][:], We[e].rearrange("(k p) f -> p k f", p=P)).then_inc(we_in[i % 2], 16)
            sp.wait_ge(z_out, 16 * NQ * B)

            def load_z(n, t):
                if not early(n):
                    sp.wait_ge(trz_done, n - 1)
                sp.dma_start(ZR[t][:], z_d[bass.ds(n * P, P), :]).then_inc(zr_in[t], 16)

            def load_x1(n, t):
                if not early(n):
                    sp.wait_ge(out_done[t], 16 * (n // 2) if isinstance(n, int) else 8 * (n - t))
                sp.dma_start(X1C[t][:], x1_d[bass.ds(n * P, P), :]).then_inc(x1c_in[t], 16)

            def store_out(n, t):
                sp.wait_ge(mix_done, E * n + E)
                dst = out.rearrange("b s d -> (b s) d")[bass.ds(n * P, P), :]
                sp.dma_start(dst, X1C[t][:]).then_inc(out_done[t], 16)

            for t in range(TB):
                load_z(t, t)
                load_x1(t, t)
            with sp.Fori(0, B - 1) as b:
                for t in range(TB):
                    load_z(b * TB + t + 2, t)
                    store_out(b * TB + t, t)
                    load_x1(b * TB + t + 2, t)
            for t in range(TB):
                store_out(NT - TB + t, t)
            for t in range(TB):
                sp.wait_ge(out_done[t], 16 * B)

        @block.gpsimd
        def _(pool):
            pool.memset(ONES[:], 1.0).then_inc(const, 1)
            pool.memset(SELW[:], 1.0).then_inc(const, 1)
            pool.memset(MHALF, -0.5).then_inc(const, 1)
            pool.memset(TZ[:], 0.0).then_inc(const, 1)
            pool.wait_ge(const, 4)
            pool.affine_select(out=IDF[:], in_=ONES[:], compare_op=ALU.is_equal, fill=0.0, base=0,
                               pattern=[[-1, P]], channel_multiplier=1).then_inc(const, 1)
            pool.affine_select(out=SELW[:], in_=SELW[:], compare_op=ALU.is_ge, fill=0.0, base=QD * (P - NQ),
                               pattern=[[-QD, 2 * P - NQ]], channel_multiplier=1).then_inc(const, 1)
            pool.affine_select(out=MSK[:], in_=ONES[:, 0:B], compare_op=ALU.is_ge, fill=0.0, base=0,
                               pattern=[[-BLK, B]], channel_multiplier=1).then_inc(const, 1)
            pool.wait_ge(const, 7)
            pool.affine_select(out=SELW[:], in_=SELW[:], compare_op=ALU.is_ge, fill=0.0, base=QD - 1 - QD * (P - NQ),
                               pattern=[[QD, 2 * P - NQ]], channel_multiplier=-1)
            pool.affine_select(out=MSK[:], in_=MSK[:], compare_op=ALU.is_ge, fill=0.0, base=BLK - 1,
                               pattern=[[BLK, B]], channel_multiplier=-1)
            pool.tensor_copy(IDB[:], IDF[:]).then_inc(const, 1)
            pool.wait_ge(kss_done, 1)
            pool.tensor_scalar(KRS, KSS, 1.0 / D, RMS_EPS, ALU.mult, ALU.add).then_inc(att_pool, 1)
            pool.wait_ge(att_pool, 1)
            pool.tensor_tensor(KRS, KRS, MHALF, ALU.pow).then_inc(krs_done, 1)

            def reg(value):
                return value if isinstance(value, int) else pool.to_reg(value)

            def rstd(n, t):
                nth = reg(n + 1)
                pool.wait_ge(const, 8)
                pool.wait_ge(mv_done, nth)
                pool.tensor_scalar(RSTD[t], MV[t][:, 1:2], 1.0, RMS_EPS, ALU.mult, ALU.add).then_inc(pool_a, 1)
                pool.wait_ge(pool_a, 7 * n + 1)
                pool.tensor_tensor(RSTD[t], RSTD[t], MHALF, ALU.pow).then_inc(rstd_done, 1)

            def y_scales(n, t):
                nth = reg(n + 1)
                step5 = reg(7 * n + 4)
                step6 = reg(7 * n + 5)
                pool.wait_ge(const, 8)
                pool.wait_ge(ysq_done, nth)
                pool.tensor_scalar(YR[t], YMS[t], 1.0 / D, RMS_EPS, ALU.mult, ALU.add).then_inc(pool_a, 1)
                pool.wait_ge(pool_a, 7 * n + 2)
                pool.tensor_tensor(YR[t], YR[t], MHALF, ALU.pow).then_inc(pool_a, 1)
                pool.wait_ge(pool_a, 7 * n + 3)
                pool.wait_ge(ymax_done, nth)
                pool.tensor_tensor(YO[t], YR[t], YM[t], ALU.mult).then_inc(pool_a, 1)
                pool.wait_ge(const, 8)
                pool.wait_ge(pool_a, step5)
                pool.tensor_scalar(YO[t], YO[t], CLIP, None, ALU.max).then_inc(pool_a, 1)
                pool.wait_ge(const, 8)
                pool.wait_ge(pool_a, step6)
                pool.tensor_scalar(YO[t], YO[t], 1.0 / QMAX, None, ALU.mult).then_inc(yo_done, 1)
                pool.wait_ge(yi_done, n + 1)
                pool.tensor_tensor(YQ[t], YR[t], YI[t], ALU.mult).then_inc(yq_done, 1)
                if not early(n):
                    pool.wait_ge(silu_done, NC * (n - 1))
                    pool.wait_ge(pool_h, 7 * (n - 1))
                pool.wait_ge(yo_done, n + 1)
                pool.wait_ge(w_step, 9)
                pool.tensor_tensor(OG[t], YO[t], WMEAN[0], ALU.mult).then_inc(pool_a, 1)
                pool.tensor_tensor(OU[t], YO[t], WMEAN[1], ALU.mult).then_inc(pool_a, 1)

            def h_scales(n, t):
                nth = reg(n + 1)
                y_steps = reg(7 * (n + 1))
                step2 = reg(7 * n + 1)
                step6 = reg(7 * n + 5)
                step7 = reg(7 * n + 6)
                pool.wait_ge(const, 8)
                pool.wait_ge(hsq_done, nth)
                pool.wait_ge(pool_a, y_steps)
                pool.tensor_scalar(HR[t], HMS[t], OU[t], OU[t], ALU.mult, ALU.mult).then_inc(pool_h, 1)
                pool.wait_ge(const, 8)
                pool.wait_ge(pool_h, step2)
                pool.tensor_scalar(HR[t], HR[t], 1.0 / FF, RMS_EPS, ALU.mult, ALU.add).then_inc(pool_h, 1)
                pool.wait_ge(pool_h, 7 * n + 2)
                pool.tensor_tensor(HR[t], HR[t], MHALF, ALU.pow).then_inc(pool_h, 1)
                pool.wait_ge(pool_h, 7 * n + 3)
                pool.tensor_tensor(HR[t], HR[t], OU[t], ALU.mult).then_inc(pool_h, 1)
                pool.wait_ge(pool_h, 7 * n + 4)
                pool.wait_ge(hmax_done, n + 1)
                pool.tensor_tensor(HO[t], HR[t], HM[t], ALU.mult).then_inc(pool_h, 1)
                pool.wait_ge(const, 8)
                pool.wait_ge(pool_h, step6)
                pool.tensor_scalar(HO[t], HO[t], CLIP, None, ALU.max).then_inc(pool_h, 1)
                pool.wait_ge(const, 8)
                pool.wait_ge(pool_h, step7)
                pool.tensor_scalar(HO[t], HO[t], 1.0 / QMAX, None, ALU.mult).then_inc(ho_done, 1)
                pool.wait_ge(hi_done, n + 1)
                pool.tensor_tensor(HQ[t], HR[t], HI[t], ALU.mult).then_inc(hq_done, 1)
                if not early(n):
                    pool.wait_ge(x1_done, n - 1)
                pool.tensor_tensor(OD[t], HO[t], WMEAN[2], ALU.mult).then_inc(pool_h, 1)

            rstd(0, 0)
            y_scales(0, 0)

            def slot(n, t, first, last):
                if not last:
                    rstd(n + 1, 1 - t)
                    y_scales(n + 1, 1 - t)
                h_scales(n, t)

            over_tiles(pool, slot)
            pool.wait_ge(x1_done, NT)
            pool.memset(BD[1][:], 0.0).then_inc(bd_zero, 1)
            for t in range(TB):
                pool.wait_ge(x1_out[t], 16 * B)
            pool.iota(IOE[:].bitcast(I32), pattern=[[0, NT], [1, E]], base=0, channel_multiplier=0).then_inc(route_p, 1)
            pool.memset(ONF[:], 1.0).then_inc(route_p, 1)
            pool.wait_ge(route_p, 2)
            pool.affine_select(out=BMK[:], in_=ONF[:, 0:2], compare_op=ALU.is_equal, fill=0.0, base=0,
                               pattern=[[-1, 2]], channel_multiplier=1).then_inc(route_p, 1)

        @block.scalar
        def _(act):
            act.dma_start(WkS[:], WkT.rearrange("(k p) d -> p k d", p=P)).then_inc(att_in, 16)
            for w, (wT, st) in enumerate(((w1T, stage0), (w2T, stage1))):
                for c in range(KD):
                    act.dma_start(st[:, c, :], wT[P * c:P * c + P, :]).then_inc(w_in[w][c], 16)
            act.dma_start(WoS[:], WoT.rearrange("(k p) d -> p k d", p=P)).then_inc(wo_in, 16)

            def weight_abs(w):
                st = stage1 if w == 1 else stage0
                for c in range(4):
                    act.wait_ge(w_in[w][c], 16)
                    if w or c:
                        act.wait_ge(w_abs, 4 * w + c)
                    nc.scalar.activation(PS[:, 0:4, :].rearrange("p a c -> p (a c)"), st[:, c, :], ACT.Abs,
                                         accum_out=WPART[:, 4 * w + c:4 * w + c + 1]).then_inc(w_abs, 1)

            weight_abs(0)
            weight_abs(1)
            act.wait_ge(repr_T, 1)
            nc.scalar.copy(RT[:].rearrange("p k m -> p (k m)"), bank[7]).then_inc(repr_Tev, 1)
            act.wait_ge(keys_done, 1)
            nc.scalar.activation(KJ[:], bank[5], ACT.Square, accum_out=KSS).then_inc(kss_done, 1)
            act.wait_ge(soft_v, 2)
            nc.scalar.activation(EROW[:, P:2 * P], EROW[:, 0:P], ACT.Exp).then_inc(soft_e, 1)
            act.wait_ge(att_pe, 1)
            nc.scalar.copy(ATT[:], bank[7][:, 256:256 + KD * B]).then_inc(att_copy, 1)
            act.wait_ge(proj_pe, 1)
            nc.scalar.copy(PROJ[0:B, :], bank[4][0:B, :]).then_inc(proj_ev, 1)
            weight_abs(2)

            def square_y(n, t):
                act.wait_ge(y_done, n + 1)
                if not early(n):
                    act.wait_ge(yq_done, n - 1)
                    act.wait_ge(hsq_done, n - 1)
                nc.scalar.activation(JUNK[:, 0:D], Y[t][:], ACT.Square, accum_out=YMS[t]).then_inc(ysq_done, 1)

            def evac_tr1(n, t):
                act.wait_ge(tr1_done, n + 1)
                nc.scalar.copy(QyT[t][:].rearrange("p k m -> p (k m)"), TY[:, 0:D]).then_inc(qyt_done, 1)

            def silu(n, t, c):
                p = NC * n + c
                act.wait_ge(g_done, p + 1)
                if c == 0:
                    act.wait_ge(pool_a, 7 * (n + 1))
                if not (isinstance(n, int) and n == 0 and c < 2):
                    act.wait_ge(hm_done, p - 1)
                nc.scalar.activation(SG[c % 2][:], GP[c % 2], ACT.Silu, scale=OG[t]).then_inc(silu_done, 1)

            def evac_tr2(n):
                for h in range(2):
                    act.wait_ge(tr2_done, 2 * n + h + 1)
                    k = KF // 2
                    nc.scalar.copy(QT[:, k * h:k * h + k, :].rearrange("p k m -> p (k m)"), TR[h]).then_inc(qt_done, 1)

            def square_h(n, t):
                act.wait_ge(hm_done, NC * (n + 1))
                act.wait_ge(ysq_done, n + 2 if not (isinstance(n, int) and n == NT - 1) else NT)
                nc.scalar.activation(JUNK[:], H[t][:], ACT.Square, accum_out=HMS[t]).then_inc(hsq_done, 1)

            square_y(0, 0)
            evac_tr1(0, 0)

            def slot(n, t, first, last):
                silu(n, t, 0)
                silu(n, t, 1)
                if not first:
                    evac_tr2(n - 1)
                silu(n, t, 2)
                silu(n, t, 3)
                if not last:
                    square_y(n + 1, 1 - t)
                square_h(n, t)
                if not last:
                    evac_tr1(n + 1, 1 - t)

            over_tiles(act, slot)
            evac_tr2(NT - 1)

            with act.Fori(0, NG // 2) as gg:
                for h in range(2):
                    for m in range(GI // 4):
                        act.wait_ge(conv_done, (2 * gg + h) * (GI // 4) + m + 1)
                        bk = bank[(h * (GI // 4) + m)]
                        nc.scalar.copy(XP[:, :, bass.ds((2 * gg + h) * GI + 4 * m, 4)],
                                       bk.rearrange("p (i a) -> p a i", i=4)).then_inc(z_done, 1)
            act.wait_ge(z_done, 4 * NG)

            def z_copy(n, t):
                if not early(n):
                    act.wait_ge(zt_pe, n - 1)
                nc.scalar.copy(ZC[t][:].rearrange("p q c -> p (q c)"),
                               XP[:, bass.ds(n * NQ, NQ), :].rearrange("p q c -> p (q c)")).then_inc(zc_done, 1)

            for t in range(TB):
                act.wait_ge(x1_out[t], 16 * B)
            z_copy(0, 0)
            z_copy(1, 1)
            with act.Fori(1, B) as b:
                z_copy(b * TB, 0)
                z_copy(b * TB + 1, 1)
            act.wait_ge(route_v, 15)
            nc.scalar.activation(EX[:], M2[:], ACT.Exp).then_inc(route_e, 1)
            for i, e in enumerate(EORD):
                act.wait_ge(we_in[i % 2], 16 * (i // 2 + 1))
                if e == EORD[4]:
                    act.wait_ge(z_out, 16 * NQ * B)
                nc.scalar.copy(WH[e][:], WST[i % 2][:]).then_inc(wh_done, 1)

            def z_high(n, t):
                act.wait_ge(trz_done, n + 1)
                if not early(n):
                    act.wait_ge(exp_done, E * (n - 1))
                nc.scalar.copy(ZH[t][:].rearrange("p k m -> p (k m)"), bank[4 + t]).then_inc(zh_done, 1)

            z_high(0, 0)
            z_high(1, 1)
            with act.Fori(1, B) as b:
                z_high(b * TB, 0)
                z_high(b * TB + 1, 1)

        @block.vector
        def _(dve):
            dve.wait_ge(att_in, 48)
            nc.vector.tensor_tensor(RW[:], RW[:], QB[:], ALU.mult).then_inc(rwq_done, 1)

            def ternary(w):
                dve.wait_ge(w_tot, w + 1)
                if w == 2:
                    dve.wait_ge(ysq_done, 1)
                nc.vector.tensor_reduce(WSUM[w], bank[6][:, 4 * w:4 * w + 4], AX.X, ALU.add).then_inc(w_step, 1)
                dve.wait_ge(w_step, 3 * w + 1)
                nc.vector.tensor_scalar(WMEAN[w], WSUM[w], 1.0 / WCOUNT, CLIP, ALU.mult, ALU.max).then_inc(w_step, 1)
                dve.wait_ge(w_step, 3 * w + 2)
                nc.vector.reciprocal(WSC[w], WMEAN[w]).then_inc(w_step, 1)
                dve.wait_ge(w_step, 3 * w + 3)
                st = stage1 if w == 1 else stage0
                for c in range(4):
                    if w == 2:
                        dst = W3[:].rearrange("p k d -> p (k d)")[:, FF * c:FF * c + FF]
                    else:
                        dst = W12[:, c, FF * w:FF * w + FF]
                    if w or c:
                        dve.wait_ge(w_tern, 4 * w + c)
                    nc.vector.tensor_scalar(TMP[:], st[:, c, :], WSC[w], 1.0, ALU.mult, ALU.min).then_inc(w_round, 1)
                    dve.wait_ge(w_round, 4 * w + c + 1)
                    nc.vector.tensor_scalar(dst, TMP[:], -1.0, None, ALU.max).then_inc(w_tern, 1)

            ternary(0)
            dve.wait_ge(repr_sum, 1)
            nc.vector.tensor_copy(R[:], bank[5]).then_inc(repr_ev, 1)
            dve.wait_ge(keys_done, 1)
            dve.wait_ge(kss_done, 1)
            dve.wait_ge(rwq_done, 1)
            nc.vector.tensor_tensor_reduce(QB[:], bank[5], RW[:], 1.0, 0.0, ALU.mult, ALU.add, DOT).then_inc(dot_done, 1)
            dve.wait_ge(dot_done, 1)
            dve.wait_ge(krs_done, 1)
            nc.vector.tensor_tensor(SCO, DOT, KRS, ALU.mult).then_inc(sco_done, 1)
            dve.wait_ge(row_done, 1)
            row = bank[7][0:1, 0:P].rearrange("o (b k) -> o b k", k=BLK)
            nc.vector.tensor_reduce(GMX, row, AX.X, ALU.max).then_inc(soft_v, 1)
            dve.wait_ge(soft_v, 1)
            er = EROW[:, 0:P].rearrange("o (b k) -> o b k", k=BLK)
            ee = EROW[:, P:2 * P].rearrange("o (b k) -> o b k", k=BLK)
            nc.vector.tensor_tensor(er, row, GMX.rearrange("o (b k) -> o b k", k=1).broadcast_to([1, B, BLK]),
                                    ALU.subtract).then_inc(soft_v, 1)
            dve.wait_ge(soft_e, 1)
            nc.vector.tensor_reduce(GSM, ee, AX.X, ALU.add).then_inc(soft_v, 1)
            dve.wait_ge(soft_v, 3)
            nc.vector.reciprocal(GMX, GSM).then_inc(soft_v, 1)
            dve.wait_ge(soft_v, 4)
            nc.vector.tensor_tensor(ROWS[:].rearrange("o (b k) -> o b k", k=BLK), ee,
                                    GMX.rearrange("o (b k) -> o b k", k=1).broadcast_to([1, B, BLK]),
                                    ALU.mult).then_inc(soft_v, 1)
            dve.wait_ge(colT_done, 1)
            nc.vector.tensor_copy(ATC, bank[7][:, P:P + 1]).then_inc(att_v, 1)
            dve.wait_ge(att_v, 1)
            dve.wait_ge(const, 8)
            nc.vector.tensor_scalar(AMX[:], MSK[:], ATC, None, ALU.mult).then_inc(att_v, 1)
            ternary(1)

            def front_1(n, t):
                dve.wait_ge(pj_in[t], 16 * (n // 2 + 1) if isinstance(n, int) else 8 * (n - t) + 16)
                nc.vector.tensor_tensor(SUM[t][:], X[:, n, :] if isinstance(n, int) else X[:, bass.ds(n, 1), :].rearrange("p o d -> p (o d)"),
                                        PJ[t][:], ALU.add).then_inc(sum_done, 1)
                dve.wait_ge(sum_done, n + 1)
                nc.vector.bn_stats(BS[t], SUM[t][:]).then_inc(stats_done, 1)

            def front_2(n, t):
                dve.wait_ge(norm_in, 32)
                dve.wait_ge(stats_done, n + 1)
                nc.vector.bn_aggr(MV[t], BS[t]).then_inc(mv_done, 1)
                dve.wait_ge(mv_done, n + 1)
                nc.vector.scalar_tensor_tensor(out=SUM[t][:], in0=SUM[t][:], scalar=MV[t][:, 0:1], in1=GAM[:],
                                               op0=ALU.subtract, op1=ALU.mult).then_inc(gam_done, 1)

            def front_3(n, t):
                dve.wait_ge(gam_done, n + 1)
                dve.wait_ge(rstd_done, n + 1)
                if not early(n):
                    dve.wait_ge(ysq_done, n - 1)
                nc.vector.scalar_tensor_tensor(out=Y[t][:], in0=SUM[t][:], scalar=RSTD[t], in1=BET[:],
                                               op0=ALU.mult, op1=ALU.add).then_inc(y_done, 1)
                dve.wait_ge(y_done, n + 1)
                nc.vector.tensor_reduce(YM[t], Y[t][:], AX.X, ALU.max, apply_absolute_value=True).then_inc(ymax_done, 1)

            def front_4(n, t):
                dve.wait_ge(yo_done, n + 1)
                nc.vector.reciprocal(YI[t], YO[t]).then_inc(yi_done, 1)

            def front_5(n, t):
                dve.wait_ge(yq_done, n + 1)
                nc.vector.tensor_scalar(Iy[:], Y[t][:], YQ[t], QMAX, ALU.mult, ALU.min).then_inc(yint_done, 1)
                dve.wait_ge(yint_done, n + 1)
                if not early(n):
                    dve.wait_ge(tr1_done, n - 1)
                nc.vector.tensor_copy(Qy[t][:], Iy[:]).then_inc(yqt_done, 1)

            def h_mul(n, t, c):
                p = NC * n + c
                dve.wait_ge(u_done, p + 1)
                dve.wait_ge(silu_done, p + 1)
                if not early(n) and c == 0:
                    dve.wait_ge(hsq_done, n - 1)
                nc.vector.tensor_tensor(H[t][:, CH * c:CH * c + CH], SG[c % 2][:], UP[c % 2], ALU.mult).then_inc(hm_done, 1)

            def h_max(n, t):
                dve.wait_ge(hm_done, NC * (n + 1))
                nc.vector.tensor_reduce(HM[t], H[t][:], AX.X, ALU.max, apply_absolute_value=True).then_inc(hmax_done, 1)

            def h_quant(n, t):
                dve.wait_ge(ho_done, n + 1)
                nc.vector.reciprocal(HI[t], HO[t]).then_inc(hi_done, 1)
                dve.wait_ge(hq_done, n + 1)
                nc.vector.tensor_scalar(Ih[:], H[t][:], HQ[t], QMAX, ALU.mult, ALU.min).then_inc(hint_done, 1)
                dve.wait_ge(hint_done, n + 1)
                if not (isinstance(n, int) and n == 0):
                    dve.wait_ge(tr2_done, 2 * n)
                nc.vector.tensor_copy(Qh[:], Ih[:]).then_inc(qh_done, 1)

            def x1_add(n, t):
                dve.wait_ge(down_done, n + 1)
                if not early(n):
                    dve.wait_ge(x1_out[t], 16 * ((n - t) // 2) if isinstance(n, int) else 8 * (n - t))
                dve.wait_ge(pool_h, 7 * (n + 1))
                xn = X[:, n, :] if isinstance(n, int) else X[:, bass.ds(n, 1), :].rearrange("p o d -> p (o d)")
                nc.vector.scalar_tensor_tensor(out=X1[t][:], in0=DN, scalar=OD[t], in1=xn,
                                               op0=ALU.mult, op1=ALU.add).then_inc(x1_done, 1)

            dve.wait_ge(norm_in, 32)
            front_1(0, 0)
            front_2(0, 0)
            front_3(0, 0)
            front_4(0, 0)
            front_5(0, 0)
            ternary(2)

            def slot(n, t, first, last):
                h_mul(n, t, 0)
                if not last:
                    front_1(n + 1, 1 - t)
                h_mul(n, t, 1)
                if not last:
                    front_2(n + 1, 1 - t)
                h_mul(n, t, 2)
                if not last:
                    front_3(n + 1, 1 - t)
                h_mul(n, t, 3)
                if not last:
                    front_4(n + 1, 1 - t)
                h_max(n, t)
                if not last:
                    front_5(n + 1, 1 - t)
                h_quant(n, t)
                if not first:
                    x1_add(n - 1, 1 - t)

            over_tiles(dve, slot)
            x1_add(NT - 1, 1)

            nc.vector.memset(BD[0][:], 0.0).then_inc(bd_zero, 1)
            dve.wait_ge(bd_zero, 2)
            dve.wait_ge(T_in, 16 * NQ)

            def spread(g, h, first):
                if not first:
                    dve.wait_ge(conv_done, (g - 1) * (GI // 4))
                for j in range(NQ):
                    q = slice(QD * j, QD * j + QD)
                    i = nc.vector.tensor_copy(BD[h][q, :, :, q][:, :, :, ::-1],
                                             
                                              T[q, bass.ds(g * GI, GI), :].rearrange("p i (w u) -> p w i u", w=2))
                i.then_inc(bd_done, 1)

            spread(0, 0, True)
            spread(1, 1, True)
            with dve.Fori(1, NG // 2) as gg:
                spread(2 * gg, 0, False)
                spread(2 * gg + 1, 1, False)

            for t in range(TB):
                dve.wait_ge(x1_out[t], 16 * B)

            def z_turned(n, t):
                dve.wait_ge(zt_pe, n + 1)
                if not early(n):
                    dve.wait_ge(lg_done, n - 1)
                nc.vector.tensor_copy(ZT[t][:].rearrange("p j (q u) -> p q j u", q=NQ),
                                      bank[4 + t].rearrange("p (q j u) -> p q j u", q=NQ, j=NQ)).then_inc(zt_done, 1)

            z_turned(0, 0)
            z_turned(1, 1)
            with dve.Fori(1, B) as b:
                z_turned(b * TB, 0)
                z_turned(b * TB + 1, 1)

            def wide(m):
                return m[:].rearrange("p (n o) -> p n o", o=1).broadcast_to([P, NT, E])

            step = [0]

            def v(i):
                step[0] += 1
                i.then_inc(route_v, 1)
                dve.wait_ge(route_v, step[0])

            dve.wait_ge(lg_done, NT)
            dve.wait_ge(route_p, 1)
            v(nc.vector.tensor_copy(CAND[:], IOE[:].bitcast(I32)))
            v(nc.vector.tensor_scalar(IOE[:], CAND[:], -float(E), None, ALU.add))
            v(nc.vector.tensor_copy(LG[:].rearrange("p n e -> p (n e)"), bank[6][:, 0:NR]))
            v(nc.vector.tensor_reduce(M1[:], LG[:], AX.X, ALU.max))
            v(nc.vector.tensor_tensor(OH1[:], LG[:], wide(M1), ALU.is_equal))
            v(nc.vector.tensor_tensor(CAND[:], OH1[:], IOE[:], ALU.mult))
            v(nc.vector.tensor_reduce(S1[:], CAND[:], AX.X, ALU.min))
            v(nc.vector.tensor_tensor(OH1[:], IOE[:], wide(S1), ALU.is_equal))
            v(nc.vector.scalar_tensor_tensor(out=L2[:], in0=OH1[:], scalar=-3e38, in1=LG[:], op0=ALU.mult, op1=ALU.add))
            v(nc.vector.tensor_reduce(M2[:], L2[:], AX.X, ALU.max))
            v(nc.vector.tensor_tensor(OH2[:], L2[:], wide(M2), ALU.is_equal))
            v(nc.vector.tensor_tensor(CAND[:], OH2[:], IOE[:], ALU.mult))
            v(nc.vector.tensor_reduce(S2[:], CAND[:], AX.X, ALU.min))
            v(nc.vector.tensor_tensor(OH2[:], IOE[:], wide(S2), ALU.is_equal))
            v(nc.vector.tensor_tensor(M2[:], M2[:], M1[:], ALU.subtract))
            dve.wait_ge(route_e, 1)
            v(nc.vector.tensor_scalar(P1[:], EX[:], 1.0, None, ALU.add))
            v(nc.vector.reciprocal(P1[:], P1[:]))
            v(nc.vector.tensor_tensor(P2[:], P1[:], EX[:], ALU.mult))
            v(nc.vector.tensor_tensor(OH1[:], OH1[:], wide(P1), ALU.mult))
            v(nc.vector.tensor_tensor(OH2[:], OH2[:], wide(P2), ALU.mult))
            v(nc.vector.tensor_tensor(GATE[:], OH1[:].rearrange("p n e -> p (n e)"), OH2[:].rearrange("p n e -> p (n e)"), ALU.add))
            dve.wait_ge(be_in, 16)
            dve.wait_ge(route_p, 3)
            nc.vector.tensor_copy(ONR[:], ONF[:]).then_inc(be_done, 1)
            nc.vector.tensor_copy(BEP[:], BEV[:]).then_inc(be_done, 1)
            dve.wait_ge(be_done, 2)
            nc.vector.tensor_tensor(BEV[:], BEV[:], BEP[:].bitcast(F32), ALU.subtract).then_inc(be_done, 1)
            dve.wait_ge(be_done, 3)
            nc.vector.tensor_scalar(BEV[:], BEV[:], BMK[:, 1:2], None, ALU.mult).then_inc(be_done, 1)
            dve.wait_ge(be_done, 4)
            nc.vector.scalar_tensor_tensor(out=BEP[:], in0=BEP[:].bitcast(F32), scalar=BMK[:, 0:1], in1=BEV[:],
                                           op0=ALU.mult, op1=ALU.add).then_inc(be_done, 1)
            for i, e in enumerate(EORD):
                dve.wait_ge(wh_done, i + 1)
                nc.vector.tensor_tensor(WL[e][:], WST[i % 2][:], WH[e][:].bitcast(F32), ALU.subtract).then_inc(wl_done, 1)

            def z_low(n, t):
                dve.wait_ge(zh_done, n + 1)
                if not early(n):
                    dve.wait_ge(exp_done, E * (n - 1))
                nc.vector.tensor_tensor(ZL[t][:].rearrange("p k m -> p (k m)"), bank[4 + t],
                                        ZH[t][:].rearrange("p k m -> p (k m)").bitcast(F32), ALU.subtract).then_inc(zl_done, 1)

            def mix(n, t):
                for e in range(E):
                    dve.wait_ge(exp_done, E * n + e + 1)
                    if e == 0:
                        dve.wait_ge(x1c_in[t], 16 * (n // 2 + 1) if isinstance(n, int) else 8 * (n - t) + 16)
                    else:
                        dve.wait_ge(mix_done, E * n + e)
                    nc.vector.scalar_tensor_tensor(out=X1C[t][:], in0=bank[e % 4], scalar=GATE[:, bass.ds(n * E + e, 1)],
                                                   in1=X1C[t][:], op0=ALU.mult, op1=ALU.add).then_inc(mix_done, 1)

            z_low(0, 0)
            z_low(1, 1)
            mix(0, 0)
            z_low(2, 0)
            mix(1, 1)
            with dve.Fori(1, B - 1) as b:
                for t in range(TB):
                    z_low(b * TB + t + 1, 1 - t)
                    mix(b * TB + t, t)
            z_low(NT - 1, 1)
            mix(NT - 2, 0)
            mix(NT - 1, 1)

        @block.tensor
        def _(pe):
            pe.wait_ge(const, 8)
            for n in range(NT):
                if n % (NT // 8) == 0:
                    pe.wait_ge(x_in[n // (NT // 8)], 16)
                o = P - NQ - NQ * n
                i = nc.tensor.matmul(bank[5], SELW[:, o:o + P], X[:, n, :], start=(n == 0), stop=(n == NT - 1))
            i.then_inc(repr_sum, 1)

            def weight_total(w):
                pe.wait_ge(w_abs, 4 * w + 4)
                if w:
                    pe.wait_ge(w_step, 3 * w - 2)
                nc.tensor.matmul(bank[6][:, 4 * w:4 * w + 4], ONES[:], WPART[:, 4 * w:4 * w + 4],
                                 start=True, stop=True).then_inc(w_tot, 1)

            weight_total(0)
            pe.wait_ge(repr_ev, 1)
            for k in range(KD):
                i = nc.tensor.transpose(bank[7][:, P * k:P * k + P], R[:, P * k:P * k + P], IDF[:])
            i.then_inc(repr_T, 1)
            pe.wait_ge(repr_Tev, 1)
            pe.wait_ge(att_in, 48)
            for k in range(KD):
                i = nc.tensor.matmul(bank[5], RT[:, k, :], WkS[:, k, :], start=(k == 0), stop=(k == KD - 1))
            i.then_inc(keys_done, 1)
            pe.wait_ge(sco_done, 1)
            nc.tensor.matmul(bank[7][0:1, 0:P], SCO, IDF[:], start=True, stop=True).then_inc(row_done, 1)
            pe.wait_ge(soft_v, 5)
            nc.tensor.matmul(bank[7][:, P:P + 1], ROWS[:], ONES[0:1, 0:1], start=True, stop=True).then_inc(colT_done, 1)
            pe.wait_ge(att_v, 2)
            for k in range(KD):
                i = nc.tensor.matmul(bank[7][:, 256 + B * k:256 + B * k + B], R[:, P * k:P * k + P], AMX[:],
                                     start=True, stop=True)
            i.then_inc(att_pe, 1)
            pe.wait_ge(att_copy, 1)
            pe.wait_ge(wo_in, 16)
            for k in range(KD):
                i = nc.tensor.matmul(bank[4][0:B, :], ATT[:, B * k:B * k + B], WoS[:, k, :],
                                     start=(k == 0), stop=(k == KD - 1))
            i.then_inc(proj_pe, 1)
            weight_total(1)
            weight_total(2)

            def turn_y(n, t):
                pe.wait_ge(yqt_done, n + 1)
                if not (isinstance(n, int) and n == 0):
                    pe.wait_ge(qyt_done, n)
                for k in range(KD):
                    i = nc.tensor.transpose(TY[:, P * k:P * k + P], Qy[t][:, P * k:P * k + P], IDB[:])
                i.then_inc(tr1_done, 1)

            def up(n, t, c):
                p = NC * n + c
                if c == 0:
                    pe.wait_ge(qyt_done, n + 1)
                free = not (isinstance(n, int) and n == 0 and c < 2)
                if free:
                    pe.wait_ge(silu_done, p - 1)
                for k in range(KD):
                    i = nc.tensor.matmul(GP[c % 2], QyT[t][:, k, :], W12[:, k, CH * c:CH * c + CH],
                                         start=(k == 0), stop=(k == KD - 1))
                i.then_inc(g_done, 1)
                if free:
                    pe.wait_ge(hm_done, p - 1)
                for k in range(KD):
                    i = nc.tensor.matmul(UP[c % 2], QyT[t][:, k, :], W12[:, k, FF + CH * c:FF + CH * c + CH],
                                         start=(k == 0), stop=(k == KD - 1))
                i.then_inc(u_done, 1)

            def turn_h(n):
                pe.wait_ge(qh_done, n + 1)
                for h in range(2):
                    if not (isinstance(n, int) and n == 0):
                        pe.wait_ge(qt_done, 2 * n + h - 1)
                    for k in range(KF // 2):
                        kk = KF // 2 * h + k
                        i = nc.tensor.transpose(TR[h][:, P * k:P * k + P], Qh[:, P * kk:P * kk + P], IDB[:])
                    i.then_inc(tr2_done, 1)

            def down(n):
                if not (isinstance(n, int) and n == 0):
                    pe.wait_ge(x1_done, n)
                for k in range(KF):
                    if k % (KF // 2) == 0:
                        pe.wait_ge(qt_done, 2 * n + k // (KF // 2) + 1)
                    i = nc.tensor.matmul(DN, QT[:, k, :], W3[:, k, :], start=(k == 0), stop=(k == KF - 1))
                i.then_inc(down_done, 1)

            turn_y(0, 0)
            pe.wait_ge(w_tern, 12)

            def slot(n, t, first, last):
                up(n, t, 0)
                up(n, t, 1)
                if not first:
                    turn_h(n - 1)
                up(n, t, 2)
                up(n, t, 3)
                if not first:
                    down(n - 1)
                if not last:
                    turn_y(n + 1, 1 - t)

            over_tiles(pe, slot)
            turn_h(NT - 1)
            down(NT - 1)

            pe.wait_ge(xp_in, 16 * NQ * B)
            pe.wait_ge(x1_done, NT)

            def conv(g, h, first):
                pe.wait_ge(bd_done, g + 1)
                for i in range(GI):
                    m = i // 4
                    if i % 4 == 0 and not first:
                        pe.wait_ge(z_done, (g - 2) * (GI // 4) + m + 1)
                    o = bank[h * (GI // 4) + m][:, NBLK * (i % 4):NBLK * (i % 4) + NBLK]
                    xi = XP[:, :, bass.ds(g * GI + i, 1)].rearrange("p a o -> p (a o)")
                    nc.tensor.matmul(o, BD[h][:, 1, i, :], xi, start=True, stop=False)
                    mm = nc.tensor.matmul(o.rearrange("p (b k) -> p b k", k=BLK)[:, :, 1:BLK], BD[h][:, 0, i, :],
                                          xi.rearrange("p (b k) -> p b k", k=BLK)[:, :, 0:BLK - 1],
                                          start=False, stop=True)
                    if i % 4 == 3:
                        mm.then_inc(conv_done, 1)

            conv(0, 0, True)
            conv(1, 1, True)
            with pe.Fori(1, NG // 2) as gg:
                conv(2 * gg, 0, False)
                conv(2 * gg + 1, 1, False)

            pe.wait_ge(z_done, 4 * NG)
            pe.wait_ge(route_in, 16)

            def turn_z(n, t):
                pe.wait_ge(zc_done, n + 1)
                if not early(n):
                    pe.wait_ge(zt_done, n - 1)
                for q in range(NQ):
                    i = nc.tensor.transpose(bank[4 + t][:, P * q:P * q + P], ZC[t][:, q, :], IDF[:])
                i.then_inc(zt_pe, 1)

            def logits(n, t):
                pe.wait_ge(zt_done, n + 1)
                for j in range(NQ):
                    i = nc.tensor.matmul(bank[6][:, bass.ds(n * E, E)], ZT[t][:, j, :], WRS[:, j, :],
                                         start=(j == 0), stop=(j == NQ - 1))
                i.then_inc(lg_done, 1)

            turn_z(0, 0)
            turn_z(1, 1)
            logits(0, 0)
            turn_z(2, 0)
            logits(1, 1)
            with pe.Fori(1, B - 1) as b:
                for t in range(TB):
                    turn_z(b * TB + t + 1, 1 - t)
                    logits(b * TB + t, t)
            turn_z(NT - 1, 1)
            logits(NT - 2, 0)
            logits(NT - 1, 1)

            def turn_r(n, t):
                pe.wait_ge(zr_in[t], 16 * (n // 2 + 1) if isinstance(n, int) else 8 * (n - t) + 16)
                if not early(n):
                    pe.wait_ge(zl_done, n - 1)
                for k in range(KD):
                    i = nc.tensor.transpose(bank[4 + t][:, P * k:P * k + P], ZR[t][:, P * k:P * k + P], IDF[:])
                i.then_inc(trz_done, 1)

            def experts(n, t):
                pe.wait_ge(zl_done, n + 1)
                for e in range(E):
                    if not (isinstance(n, int) and n == 0 and e < 4):
                        pe.wait_ge(mix_done, E * n + e - 3)
                    for k in range(KD):
                        for m, (zz, ww) in enumerate(((ZH, WH), (ZH, WL), (ZL, WH))):
                            nc.tensor.matmul(bank[e % 4], zz[t][:, k, :], ww[e][:, k, :], start=(k == 0 and m == 0), stop=False)
                    nc.tensor.matmul(bank[e % 4], ONR[:], BEP[:, D * e:D * e + D], start=False, stop=True).then_inc(exp_done, 1)

            pe.wait_ge(lg_done, NT)
            turn_r(0, 0)
            pe.wait_ge(be_done, 5)
            pe.wait_ge(wl_done, E)
            turn_r(1, 1)
            experts(0, 0)
            turn_r(2, 0)
            experts(1, 1)
            with pe.Fori(1, B - 1) as b:
                for t in range(TB):
                    turn_r(b * TB + t + 1, 1 - t)
                    experts(b * TB + t, t)
            turn_r(NT - 1, 1)
            experts(NT - 2, 0)
            experts(NT - 1, 1)


def kernel(**inputs):
    import numpy as np
    import concourse.bacc as bacc
    from concourse.bass_utils import run_bass_kernel_spmd

    arrays = {
        "x": inputs["x"],
        "cond": inputs["cond_2048"],
        "taps": np.asarray(inputs["cond_2048"]).T,
        "rms_w": inputs["L0_cond_rms_weight"],
        "WkT": np.asarray(inputs["L0_cond_Wk"]).T,
        "WoT": np.asarray(inputs["L0_cond_Wo"]).T,
        "gamma": inputs["L0_cond_ln_gamma"],
        "beta": inputs["L0_cond_ln_beta"],
        "w1T": np.asarray(inputs["L0_ffn_w1"]).T,
        "w2T": np.asarray(inputs["L0_ffn_w2"]).T,
        "w3T": np.asarray(inputs["L0_ffn_w3"]).T,
        "Wr": inputs["L1_ffn_Wr"],
        "We": inputs["L1_ffn_We"],
        "be": inputs["L1_ffn_be"],
    }
    nc = bacc.Bacc("TRN2", target_bir_lowering=False, num_devices=1)
    feed, args = {}, []
    for name, a in arrays.items():
        a = np.ascontiguousarray(a)
        feed[f"in_{name}"] = a
        args.append(nc.dram_tensor(f"in_{name}", a.shape, mybir.dt.from_np(a.dtype), kind="ExternalInput").ap())
    out = nc.dram_tensor("out_x", tuple(arrays["x"].shape), F32, kind="ExternalOutput").ap()
    adaln_ffn_moe(nc, *args, out)
    r = run_bass_kernel_spmd(nc, [feed], core_ids=[0])
    return r.results[0]["out_x"]
```

```python
from contextlib import ExitStack

import concourse.bass as bass
from concourse import mybir

F32 = mybir.dt.float32
F32R = mybir.dt.float32r
BF16 = mybir.dt.bfloat16
I16 = mybir.dt.int16
I32 = mybir.dt.int32
U32 = mybir.dt.uint32
ALU = mybir.AluOpType
ACT = mybir.ActivationFunctionType
AX = mybir.AxisListType

P = 128
QD = 32
NQ = P // QD
QMAX = 127.0
CLIP = 1e-5
RMS_EPS = 1e-6


def adaln_ffn_moe(nc, x, cond, taps, rms_w, WkT, WoT, gamma, beta, w1T, w2T, w3T, Wr, We, be, out):
    B, S, D = x.shape
    FF = w1T.shape[1]
    E = We.shape[0]
    K = taps.shape[1]
    TOK = B * S
    NT = TOK // P
    TB = S // P
    BLK = 8
    NBLK = B * BLK
    KD = D // P
    KF = FF // P
    CH = 512
    NC = FF // CH
    NI = D // NQ
    GI = 16
    NG = NI // GI
    WIN = 2 * QD
    PADW = 3 * QD
    WCOUNT = float(D * FF)
    NK = 2 * NT
    MT = NK + E
    UN = 4
    NGR = NT // UN
    CC = NK // 4
    assert MT % UN == 0
    assert S // BLK == QD and TB == 2 and KD == NQ and NBLK == P and K <= QD and D == CH

    ctx = ExitStack()
    with ctx:
        def sem(name):
            return ctx.enter_context(nc.semaphore(name))

        def dram(name, shape):
            return nc.dram_tensor(name, shape, F32, kind="Internal").ap()

        proj_d = dram("proj_scratch", (B, D))
        taps_d = dram("taps_scratch", (D, PADW))
        x1_d = dram("x1_scratch", (TOK, D))
        z_d = dram("z_scratch", (TOK, D))
        y_d = dram("y_scratch", (2 * TOK + (2 * TOK // P + E) * P, D))

        base = (nc.sbuf_base + 31) // 32 * 32
        words = (nc.sbuf_usable_end - base) // 4

        def place(name, at, shape, dt=F32):
            n = 4 if dt in (F32, F32R) else 2
            size = n
            for s in shape[1:]:
                size *= s
            assert at >= 0 and at + size // 4 <= words, (name, at, size, words)
            return nc.alloc_sbuf_tensor_at(name, list(shape), dt, offset=base + 4 * at)

        a_x, a_w12, a_w3, a_T = 0, NT * D, NT * D + KD * FF, NT * D + KD * FF + KF * D // 2
        a_h = a_T + NI * WIN
        X = place("X", a_x, [P, NT, D])
        XP = place("XP", a_x, [P, NBLK, NI])
        W12 = place("W12", a_w12, [P, KD, 2 * FF], BF16)
        W3 = place("W3", a_w3, [P, KF, D], BF16)
        T = place("T", a_T, [P, NI, WIN])
        stage0 = place("stage0", a_T, [P, 4, FF])
        stage1 = place("stage1", a_h, [P, 4, FF])
        H = [place(f"H{i}", a_h + FF * i, [P, FF]) for i in range(2)]
        a = a_h + 2 * FF
        QT = place("QT", a, [P, KF, P], BF16)
        Qh = place("Qh", a + FF // 2, [P, FF], BF16)
        SG = [place(f"SG{i}", a + FF + CH * i, [P, CH]) for i in range(2)]
        Ih = place("Ih", a + FF + 2 * CH, [P, FF], I16)
        BD = [place(f"BD{i}", a_h + 2 * GI * P * i, [P, 2, GI, P]) for i in range(2)]
        a_s = a_h + 4 * FF
        assert a + FF + 2 * CH + FF // 2 <= a_s
        SUM = [place(f"SUM{i}", a_s + D * i, [P, D]) for i in range(2)]
        Y = [place(f"Y{i}", a_s + D * (2 + i), [P, D]) for i in range(2)]
        PJ = [place(f"PJ{i}", a_s + D * (4 + i), [P, D]) for i in range(2)]
        X1 = [place(f"X1{i}", a_s + D * (6 + i), [P, D]) for i in range(2)]
        WkS = place("WkS", a_s, [P, KD, D])
        WoS = place("WoS", a_s + KD * D, [P, KD, D])
        a = a_s + 8 * D
        Iy = place("Iy", a, [P, D], I16)
        Qy = [place(f"Qy{i}", a + D // 2 * (1 + i), [P, D], BF16) for i in range(2)]
        QyT = [place(f"QyT{i}", a + D // 2 * (3 + i), [P, KD, P], BF16) for i in range(2)]
        a += D // 2 * 5
        GAM = place("GAM", a, [P, D])
        BET = place("BET", a + D, [P, D])
        JUNK = place("JUNK", a + 2 * D, [P, FF], BF16)
        TMP = place("TMP", a + 2 * D, [P, FF], I16)
        a += 2 * D + FF // 2
        TZ = place("TZ", a, [P, KD, PADW])
        a += KD * PADW
        IDF = place("IDF", a, [P, P])
        IDB = place("IDB", a + P, [P, P], BF16)
        sm = place("sm", a + P + P // 2, [P, 96])
        R = place("R", a_w3, [P, D])
        RT = place("RT", a_w3 + D, [P, KD, P])
        RW = place("RW", a_w3 + 2 * D, [P, D])
        QB = place("QB", a_w3 + 3 * D, [P, D])
        PROJ = place("PROJ", a_w3 + 4 * D, [P, D])
        KJ = place("KJ", a_w3 + 5 * D, [P, D])
        SELW = place("SELW", a_w3 + 6 * D, [P, 2 * P - NQ])
        ONES = place("ONES", a_w3 + 6 * D + 2 * P, [P, P])
        ROWS = place("ROWS", a_w3 + 6 * D + 3 * P, [1, P])
        EROW = place("EROW", a_w3 + 7 * D, [1, 3 * P])
        MSK = place("MSK", a_w3 + 7 * D + 3 * P, [P, B])
        AMX = place("AMX", a_w3 + 7 * D + 3 * P + B, [P, B])
        ATT = place("ATT", a_w3 + 7 * D + 3 * P + 2 * B, [P, KD * B])
        DOT, KSS, KRS, SCO, ATC = (sm[:, 64 + i:65 + i] for i in range(5))
        GMX, GSM = sm[0:1, 70:70 + B], EROW[:, 2 * P:2 * P + B]

        def col(i):
            return [sm[:, 2 * i + t:2 * i + t + 1] for t in range(2)]

        YMS, YR, YM, YO, YI, YQ, OG, OU = (col(i) for i in range(8))
        HMS, HR, HM, HO, HI, HQ, OD, RSTD = (col(8 + i) for i in range(8))
        MV = [sm[:, 32 + 2 * t:34 + 2 * t] for t in range(2)]
        BS = [sm[:, 36 + 6 * t:42 + 6 * t] for t in range(2)]
        WSUM, WMEAN, WSC = ([sm[:, 48 + 3 * i + w:49 + 3 * i + w] for w in range(3)] for i in range(3))
        MHALF = sm[:, 57:58]
        WPART = place("WPART", a_w3 + 7 * D + 3 * P + 2 * B + KD * B, [P, 12])

        NEXP = KD * D
        W2 = place("W2", 0, [P, E, 2, KD, D], F32R)

        def where(e):
            return (e + E // 2) % E

        WRAW = [place(f"WRAW{e}", (2 * where(e) + 1) * NEXP, [P, KD, D]) for e in range(E)]
        a = a_T + NI * WIN // 2
        assert a == 2 * E * NEXP and CC * P <= UN * D and a + 2 * UN * D <= a_h
        AOH = [place(f"AOH{i}", a + CC * P // 2 * i, [P, CC, P], BF16) for i in range(2)]
        ZR = [place(f"ZR{i}", a + UN * D + D * i, [P, D]) for i in range(UN)]
        YS = [place(f"YS{i}", a_h + D * i, [P, D]) for i in range(UN)]
        ZH = [place(f"ZH{i}", a_h + D * (UN + i), [P, KD, P], F32R) for i in range(2)]
        ZL = [place(f"ZL{i}", a_h + D * (UN + 2 + i), [P, KD, P], F32R) for i in range(2)]
        BEB = place("BEB", a_h + 8 * D, [P, E, D])
        X1C = place("X1C", 0, [P, NT, D])
        YC = [[place(f"YC{i}_{k}", NT * D + (2 * i + k) * UN * D, [P, UN, D]) for k in range(2)] for i in range(NGR // 2)]
        a = a_s
        ZC = [place(f"ZC{i}", a + D * i, [P, NQ, NI]) for i in range(2)]
        ZT = [place(f"ZT{i}", a + D * (2 + i), [P, NQ, NI]) for i in range(2)]
        BOH = [place(f"BOH{i}", a + CC * MT * i, [P, CC, 2, MT], BF16) for i in range(2)]
        a += CC * MT * 2
        GE = place("GE", a, [1, MT, E])
        a += MT * E
        MW = (MT + 7) // 8 * 8
        TEF, TEK, TSUM, TPAD, TTOK = (place(n, a + MW * i, [1 if i < 2 else P, MT]) for i, n in
                                      enumerate(("TEF", "TEK", "TSUM", "TPAD", "TTOK")))
        a += 5 * MW
        TEXP, TPLC, IDG, IDS = (place(n, a + MW * i, [1 if i < 2 else P, MT], I32) for i, n in
                                enumerate(("TEXP", "TPLC", "IDG", "IDS")))
        a += 4 * MW
        IXG, IXS = ([place(f"{n}{i}", a + 8 * (UN * j + i), [P, 1], I32) for i in range(UN)] for j, n in enumerate(("IXG", "IXS")))
        a += 16 * UN
        PADI = place("PADI", a, [P, MT], I32)
        PADF = place("PADF", a + MW, [P, MT])
        assert a + 2 * MW <= a_s + 8 * D
        NR = NT * E
        LG, L2, OH1, OH2, CAND, IOE = (place(n, a_s + 8 * D + NR * i, [P, NT, E]) for i, n in
                                       enumerate(("LG", "L2", "OH1", "OH2", "CAND", "IOE")))
        SA, SB = LG, L2
        a = a_s + 8 * D + 6 * NR
        M1, M2, S1, S2, EX, P1, P2 = (place(n, a + NT * i, [P, NT]) for i, n in
                                      enumerate(("M1", "M2", "S1", "S2", "EX", "P1", "P2")))
        a += 7 * NT
        WRS = place("WRS", a, [P, KD, E])
        a += KD * E
        CNT = place("CNT", a, [P, NT, E], BF16)
        TRI, ONB, IOSB = (place(n, a + NR // 2 + P // 2 * i, [P, P], BF16) for i, n in enumerate(("TRI", "ONB", "IOSB")))
        a += NR // 2 + 3 * P // 2
        IOS = place("IOS", a, [P, P], I32)
        IOSF = place("IOSF", a + P, [P, P])
        a += 2 * P
        TEI = place("TEI", a, [P, E], I32)
        TE, ENDA, ENDB, STA = (place(n, a + E * (1 + i), [P, E]) for i, n in enumerate(("TE", "ENDA", "ENDB", "STA")))
        PIDI = place("PIDI", a + 5 * E, [P, 1], I32)
        PIDX = place("PIDX", a + 6 * E, [P, 1])
        a += 7 * E
        POS, MTF = (place(n, a + NK * i, [P, NK]) for i, n in enumerate(("POS", "MTF")))
        MTI = place("MTI", a + 2 * NK, [P, NK], I32)
        SLB, MTB = (place(n, a + 3 * NK + NK // 2 * i, [P, NK], BF16) for i, n in enumerate(("SLB", "MTB")))
        a += 4 * NK
        assert a <= a_s + 8 * D + 5 * (D // 2) + 2 * D + FF // 2 + KD * PADW

        PS = ctx.enter_context(nc.psum_tensor("PS", [P, 8, CH], F32))
        bank = [PS[:, i, :] for i in range(8)]
        GP, UP = [bank[0], bank[2]], [bank[1], bank[3]]
        TR = [bank[4].bitcast(BF16), bank[5].bitcast(BF16)]
        DN = bank[6]
        TY = bank[7].bitcast(BF16)

        x_in = [sem(f"x_in{i}") for i in range(8)]
        att_in, wo_in, norm_in, taps_in, taps_out = sem("att_in"), sem("wo_in"), sem("norm_in"), sem("taps_in"), sem("taps_out")
        w_in = [[sem(f"w_in{w}_{c}") for c in range(4)] for w in range(3)]
        T_in, proj_out = sem("T_in"), sem("proj_out")
        pj_in = [sem(f"pj_in{t}") for t in range(2)]
        x1_out = [sem(f"x1_out{t}") for t in range(2)]
        xp_in, z_out = sem("xp_in"), sem("z_out")
        const = sem("const")
        repr_sum, repr_ev, repr_T, repr_Tev, keys_done = sem("repr_sum"), sem("repr_ev"), sem("repr_T"), sem("repr_Tev"), sem("keys_done")
        rwq_done, kss_done, dot_done, krs_done = sem("rwq_done"), sem("kss_done"), sem("dot_done"), sem("krs_done")
        sco_done, row_done, soft_v, soft_e, colT_done = sem("sco_done"), sem("row_done"), sem("soft_v"), sem("soft_e"), sem("colT_done")
        att_v, att_pe, att_copy, proj_pe, proj_ev = sem("att_v"), sem("att_pe"), sem("att_copy"), sem("proj_pe"), sem("proj_ev")
        att_pool = sem("att_pool")
        w_abs, w_tot, w_step, w_round, w_tern = (sem(n) for n in ("w_abs", "w_tot", "w_step", "w_round", "w_tern"))
        sum_done, stats_done, mv_done, gam_done, y_done, ymax_done = (sem(n) for n in ("sum_done", "stats_done", "mv_done", "gam_done", "y_done", "ymax_done"))
        ysq_done, rstd_done, yo_done, yi_done, yq_done = (sem(n) for n in ("ysq_done", "rstd_done", "yo_done", "yi_done", "yq_done"))
        yint_done, yqt_done, tr1_done, qyt_done = (sem(n) for n in ("yint_done", "yqt_done", "tr1_done", "qyt_done"))
        pool_a = sem("pool_a")
        g_done, u_done, silu_done, hm_done = (sem(n) for n in ("g_done", "u_done", "silu_done", "hm_done"))
        hsq_done, hmax_done, ho_done, hi_done, hq_done = (sem(n) for n in ("hsq_done", "hmax_done", "ho_done", "hi_done", "hq_done"))
        pool_h = sem("pool_h")
        hint_done, qh_done, tr2_done, qt_done, down_done, x1_done = (sem(n) for n in ("hint_done", "qh_done", "tr2_done", "qt_done", "down_done", "x1_done"))
        bd_zero, bd_done, conv_done, z_done = sem("bd_zero"), sem("bd_done"), sem("conv_done"), sem("z_done")
        zc_done, zt_pe, zt_done, lg_done = sem("zc_done"), sem("zt_pe"), sem("zt_done"), sem("lg_done")
        route_in, route_v, route_e = sem("route_in"), sem("route_v"), sem("route_e")
        route_p, cnt_done, pre_done = sem("route_p"), sem("cnt_done"), sem("pre_done")
        oh_done, tab_done, slots_done = sem("oh_done"), sem("tab_done"), sem("slots_done")
        we_in = [sem(f"we_in{e}") for e in range(E // 2)]
        wh_done, wl_pool, wl_dve, be_in = sem("wh_done"), sem("wl_pool"), sem("wl_dve"), sem("be_in")
        ix_done = sem("ix_done")
        zr_in = [sem(f"zr_in{i}") for i in range(UN)]
        y_out = [sem(f"y_out{i}") for i in range(UN)]
        trz_done, zh_done, zl_done, exp_done, ys_done = (sem(n) for n in ("trz_done", "zh_done", "zl_done", "exp_done", "ys_done"))
        x1c_in, yc_in = ([sem(f"{n}{i}") for i in range(NGR // 2)] for n in ("x1c_in", "yc_in"))
        out_done = sem("out_done")
        mix_a, mix_done = sem("mix_a"), sem("mix_done")

        block = ctx.enter_context(nc.Block())

        def over_tiles(eng, slot):
            for n in range(2 * TB):
                slot(n, n % TB, n == 0, False)
            with eng.Fori(2, B - 1) as b:
                for t in range(TB):
                    slot(b * TB + t, t, False, False)
            for t in range(TB):
                slot(NT - TB + t, t, False, t == TB - 1)

        def early(n):
            return isinstance(n, int) and n < 2

        def over_slots(eng, slot):
            for m in range(UN):
                slot(m, m, True, False)
            with eng.Fori(1, MT // UN - 1) as g:
                for i in range(UN):
                    slot(g * UN + i, i, False, False)
            for m in range(MT - UN, MT):
                slot(m, m % UN, False, True)

        EP = 5

        @block.sync
        def _(sp):
            sp.dma_start(RW[:], bass.AP(rms_w.tensor, 0, [[0, P], [1, D]])).then_inc(att_in, 16)
            sp.dma_start(QB[:], bass.AP(cond.tensor, D, [[0, P], [1, D]])).then_inc(att_in, 16)
            for i in range(8):
                w = NT // 8
                sp.dma_start(X[:, w * i:w * i + w, :], x.rearrange("b (u p) d -> p (b u) d", p=P)[:, w * i:w * i + w, :]) \
                    .then_inc(x_in[i], 16)
            sp.dma_start(GAM[:], bass.AP(gamma.tensor, 0, [[0, P], [1, D]])).then_inc(norm_in, 16)
            sp.dma_start(BET[:], bass.AP(beta.tensor, 0, [[0, P], [1, D]])).then_inc(norm_in, 16)
            sp.wait_ge(const, 8)
            sp.dma_start(TZ[:, :, WIN - K:WIN], taps.rearrange("(k p) u -> p k u", p=P)).then_inc(taps_in, 16)
            sp.wait_ge(taps_in, 16)
            sp.dma_start(taps_d.rearrange("(k p) u -> p k u", p=P), TZ[:]).then_inc(taps_out, 16)
            sp.wait_ge(w_tern, 4)
            for c in range(4):
                kc = KF // 4
                sp.dma_start(stage0[:, c, :], w3T.rearrange("(k p) d -> p k d", p=P)[:, kc * c:kc * c + kc, :]) \
                    .then_inc(w_in[2][c], 16)
            sp.wait_ge(proj_ev, 1)
            sp.dma_start(proj_d, PROJ[0:B, :]).then_inc(proj_out, 16)
            sp.wait_ge(proj_out, 16)

            def load_pj(n, t):
                if not early(n):
                    sp.wait_ge(sum_done, n - 1)
                b = n // TB if isinstance(n, int) else (n - t) // TB
                sp.dma_start(PJ[t][:], bass.AP(proj_d.tensor, b * D, [[0, P], [1, D]])).then_inc(pj_in[t], 16)

            def store_x1(n, t):
                sp.wait_ge(x1_done, n + 1)
                sp.dma_start(x1_d[bass.ds(n * P, P), :], X1[t][:]).then_inc(x1_out[t], 16)

            def load_xp(b):
                for t in range(TB):
                    sp.wait_ge(x1_out[t], 16 * b + 16)
                for j in range(NQ):
                    src = bass.AP(x1_d.tensor, b * S * D + j * NI, [[D, QD], [QD * D, BLK], [1, NI]])
                    sp.dma_start(XP[QD * j:QD * j + QD, bass.ds(b * BLK, BLK), :], src).then_inc(xp_in, 16)

            load_pj(0, 0)
            load_pj(1, 1)
            sp.wait_ge(w_tern, 12)
            sp.wait_ge(taps_out, 16)
            for j in range(NQ):
                src = bass.AP(taps_d.tensor, j * NI * PADW, [[1, QD], [PADW, NI], [1, WIN]])
                sp.dma_start(T[QD * j:QD * j + QD, :, :], src).then_inc(T_in, 16)
            for t in range(TB):
                load_pj(2 + t, t)
                if t:
                    store_x1(0, 0)
            with sp.Fori(1, B - 1) as b:
                load_pj(b * TB + 2, 0)
                store_x1(b * TB - 1, 1)
                load_xp(b - 1)
                load_pj(b * TB + 3, 1)
                store_x1(b * TB, 0)
            store_x1(NT - 3, 1)
            load_xp(B - 2)
            store_x1(NT - 2, 0)
            store_x1(NT - 1, 1)
            load_xp(B - 1)
            sp.dma_start(WRS[:], Wr.rearrange("(k p) e -> p k e", p=P)).then_inc(route_in, 16)
            def load_expert(e):
                sp.dma_start(WRAW[e][:], We[e].rearrange("(k p) f -> p k f", p=P)).then_inc(we_in[e % (E // 2)], 16)

            sp.wait_ge(u_done, NC * NT)
            load_expert(0)
            load_expert(1)
            sp.wait_ge(down_done, NT)
            load_expert(2)
            sp.wait_ge(bd_done, NG)
            load_expert(3)
            sp.wait_ge(z_done, 4 * NG)
            with sp.Fori(0, B) as b:
                for j in range(NQ):
                    dst = bass.AP(z_d.tensor, b * S * D + j * NI, [[D, QD], [QD * D, BLK], [1, NI]])
                    sp.dma_start(dst, XP[QD * j:QD * j + QD, bass.ds(b * BLK, BLK), :]).then_inc(z_out, 16)
            sp.dma_start(BEB[:].rearrange("p e d -> p (e d)"), bass.AP(be.tensor, 0, [[0, P], [1, E * D]])).then_inc(be_in, 16)
            sp.wait_ge(zc_done, NT)
            sp.wait_ge(z_out, 16 * NQ * B)
            sp.wait_ge(wh_done, E // 2)
            for e in range(E // 2, E):
                load_expert(e)
            sp.wait_ge(ys_done, MT)

            def rows(t, first, g):
                return t[bass.ds(first + g * UN * P, UN * P), :].rearrange("(u p) d -> p u d", p=P)

            for g in range(NGR // 2):
                sp.dma_start(X1C[:, UN * g:UN * g + UN, :], rows(x1_d, 0, g)).then_inc(x1c_in[g], 16)
            for i in range(UN):
                sp.wait_ge(y_out[i], 16 * (MT // UN))
            for g in range(NGR):
                if g >= NGR // 2:
                    sp.wait_ge(mix_done, UN * (g - NGR // 2 + 1))
                for k in range(2):
                    sp.dma_start(YC[g % (NGR // 2)][k][:], rows(y_d, k * TOK, g)).then_inc(yc_in[g % (NGR // 2)], 16)
                if g >= NGR // 2:
                    sp.dma_start(X1C[:, UN * g:UN * g + UN, :], rows(x1_d, 0, g)).then_inc(x1c_in[g % (NGR // 2)], 16)

        @block.gpsimd
        def _(pool):
            pool.memset(ONES[:], 1.0).then_inc(const, 1)
            pool.memset(SELW[:], 1.0).then_inc(const, 1)
            pool.memset(MHALF, -0.5).then_inc(const, 1)
            pool.memset(TZ[:], 0.0).then_inc(const, 1)
            pool.wait_ge(const, 4)
            pool.affine_select(out=IDF[:], in_=ONES[:], compare_op=ALU.is_equal, fill=0.0, base=0,
                               pattern=[[-1, P]], channel_multiplier=1).then_inc(const, 1)
            pool.affine_select(out=SELW[:], in_=SELW[:], compare_op=ALU.is_ge, fill=0.0, base=QD * (P - NQ),
                               pattern=[[-QD, 2 * P - NQ]], channel_multiplier=1).then_inc(const, 1)
            pool.affine_select(out=MSK[:], in_=ONES[:, 0:B], compare_op=ALU.is_ge, fill=0.0, base=0,
                               pattern=[[-BLK, B]], channel_multiplier=1).then_inc(const, 1)
            pool.wait_ge(const, 7)
            pool.affine_select(out=SELW[:], in_=SELW[:], compare_op=ALU.is_ge, fill=0.0, base=QD - 1 - QD * (P - NQ),
                               pattern=[[QD, 2 * P - NQ]], channel_multiplier=-1)
            pool.affine_select(out=MSK[:], in_=MSK[:], compare_op=ALU.is_ge, fill=0.0, base=BLK - 1,
                               pattern=[[BLK, B]], channel_multiplier=-1)
            pool.tensor_copy(IDB[:], IDF[:]).then_inc(const, 1)
            pool.wait_ge(kss_done, 1)
            pool.tensor_scalar(KRS, KSS, 1.0 / D, RMS_EPS, ALU.mult, ALU.add).then_inc(att_pool, 1)
            pool.wait_ge(att_pool, 1)
            pool.tensor_tensor(KRS, KRS, MHALF, ALU.pow).then_inc(krs_done, 1)

            def reg(value):
                return value if isinstance(value, int) else pool.to_reg(value)

            def rstd(n, t):
                nth = reg(n + 1)
                pool.wait_ge(const, 8)
                pool.wait_ge(mv_done, nth)
                pool.tensor_scalar(RSTD[t], MV[t][:, 1:2], 1.0, RMS_EPS, ALU.mult, ALU.add).then_inc(pool_a, 1)
                pool.wait_ge(pool_a, 7 * n + 1)
                pool.tensor_tensor(RSTD[t], RSTD[t], MHALF, ALU.pow).then_inc(rstd_done, 1)

            def y_scales(n, t):
                nth = reg(n + 1)
                step5 = reg(7 * n + 4)
                step6 = reg(7 * n + 5)
                pool.wait_ge(const, 8)
                pool.wait_ge(ysq_done, nth)
                pool.tensor_scalar(YR[t], YMS[t], 1.0 / D, RMS_EPS, ALU.mult, ALU.add).then_inc(pool_a, 1)
                pool.wait_ge(pool_a, 7 * n + 2)
                pool.tensor_tensor(YR[t], YR[t], MHALF, ALU.pow).then_inc(pool_a, 1)
                pool.wait_ge(pool_a, 7 * n + 3)
                pool.wait_ge(ymax_done, nth)
                pool.tensor_tensor(YO[t], YR[t], YM[t], ALU.mult).then_inc(pool_a, 1)
                pool.wait_ge(const, 8)
                pool.wait_ge(pool_a, step5)
                pool.tensor_scalar(YO[t], YO[t], CLIP, None, ALU.max).then_inc(pool_a, 1)
                pool.wait_ge(const, 8)
                pool.wait_ge(pool_a, step6)
                pool.tensor_scalar(YO[t], YO[t], 1.0 / QMAX, None, ALU.mult).then_inc(yo_done, 1)
                pool.wait_ge(yi_done, n + 1)
                pool.tensor_tensor(YQ[t], YR[t], YI[t], ALU.mult).then_inc(yq_done, 1)
                if not early(n):
                    pool.wait_ge(silu_done, NC * (n - 1))
                    pool.wait_ge(pool_h, 7 * (n - 1))
                pool.wait_ge(yo_done, n + 1)
                pool.wait_ge(w_step, 9)
                pool.tensor_tensor(OG[t], YO[t], WMEAN[0], ALU.mult).then_inc(pool_a, 1)
                pool.tensor_tensor(OU[t], YO[t], WMEAN[1], ALU.mult).then_inc(pool_a, 1)

            def h_scales(n, t):
                nth = reg(n + 1)
                y_steps = reg(7 * (n + 1))
                step2 = reg(7 * n + 1)
                step6 = reg(7 * n + 5)
                step7 = reg(7 * n + 6)
                pool.wait_ge(const, 8)
                pool.wait_ge(hsq_done, nth)
                pool.wait_ge(pool_a, y_steps)
                pool.tensor_scalar(HR[t], HMS[t], OU[t], OU[t], ALU.mult, ALU.mult).then_inc(pool_h, 1)
                pool.wait_ge(const, 8)
                pool.wait_ge(pool_h, step2)
                pool.tensor_scalar(HR[t], HR[t], 1.0 / FF, RMS_EPS, ALU.mult, ALU.add).then_inc(pool_h, 1)
                pool.wait_ge(pool_h, 7 * n + 2)
                pool.tensor_tensor(HR[t], HR[t], MHALF, ALU.pow).then_inc(pool_h, 1)
                pool.wait_ge(pool_h, 7 * n + 3)
                pool.tensor_tensor(HR[t], HR[t], OU[t], ALU.mult).then_inc(pool_h, 1)
                pool.wait_ge(pool_h, 7 * n + 4)
                pool.wait_ge(hmax_done, n + 1)
                pool.tensor_tensor(HO[t], HR[t], HM[t], ALU.mult).then_inc(pool_h, 1)
                pool.wait_ge(const, 8)
                pool.wait_ge(pool_h, step6)
                pool.tensor_scalar(HO[t], HO[t], CLIP, None, ALU.max).then_inc(pool_h, 1)
                pool.wait_ge(const, 8)
                pool.wait_ge(pool_h, step7)
                pool.tensor_scalar(HO[t], HO[t], 1.0 / QMAX, None, ALU.mult).then_inc(ho_done, 1)
                pool.wait_ge(hi_done, n + 1)
                pool.tensor_tensor(HQ[t], HR[t], HI[t], ALU.mult).then_inc(hq_done, 1)
                if not early(n):
                    pool.wait_ge(x1_done, n - 1)
                pool.tensor_tensor(OD[t], HO[t], WMEAN[2], ALU.mult).then_inc(pool_h, 1)

            rstd(0, 0)
            y_scales(0, 0)

            def slot(n, t, first, last):
                if not last:
                    rstd(n + 1, 1 - t)
                    y_scales(n + 1, 1 - t)
                h_scales(n, t)

            over_tiles(pool, slot)
            pool.wait_ge(x1_done, NT)
            pool.memset(BD[1][:], 0.0).then_inc(bd_zero, 1)
            for t in range(TB):
                pool.wait_ge(x1_out[t], 16 * B)
            pool.iota(IOE[:].bitcast(I32), pattern=[[0, NT], [1, E]], base=0, channel_multiplier=0).then_inc(route_p, 1)
            pool.iota(IOS[:], pattern=[[1, P]], base=0, channel_multiplier=0).then_inc(route_p, 1)
            pool.iota(PIDI[:], pattern=[[0, 1]], base=0, channel_multiplier=1).then_inc(route_p, 1)
            pool.iota(PADI[:], pattern=[[P, MT]], base=2 * TOK + P, channel_multiplier=1).then_inc(route_p, 1)
            pool.memset(ONB[:], 1.0).then_inc(route_p, 1)
            pool.wait_ge(route_p, 5)
            pool.affine_select(out=TRI[:], in_=ONB[:], compare_op=ALU.is_gt, fill=0.0, base=0,
                               pattern=[[1, P]], channel_multiplier=-1).then_inc(route_p, 1)
            for e in range(EP):
                pool.wait_ge(wh_done, e + 1)
                pool.tensor_tensor(W2[:, where(e), 1], WRAW[e][:], W2[:, where(e), 0].bitcast(F32), ALU.subtract).then_inc(wl_pool, 1)
            pool.wait_ge(z_out, 16 * NQ * B)

            def gather(m, i, n_ix):
                used, ready = reg(m - UN + 1) if not (isinstance(m, int) and m < UN) else None, reg(n_ix + 1)
                pool.wait_ge(slots_done, 1)
                if used is not None:
                    pool.wait_ge(trz_done, used)
                pool.tensor_copy(IXG[i][:], IDG[:, bass.ds(m, 1)]).then_inc(ix_done, 1)
                pool.wait_ge(slots_done, 1)
                pool.wait_ge(ix_done, ready)
                pool.indirect_dma_start(ZR[i][:], None, z_d, bass.IndirectOffsetOnAxis(IXG[i][:].bitcast(U32), 0)) \
                    .then_inc(zr_in[i], 16)

            def scatter(m, i, n_ix):
                before = m // UN if isinstance(m, int) else None
                sent = None if before == 0 else reg(16 * before if before is not None else 4 * (m - i))
                done, ready = reg(m + 1), reg(n_ix + 1)
                pool.wait_ge(slots_done, 1)
                if sent is not None:
                    pool.wait_ge(y_out[i], sent)
                pool.tensor_copy(IXS[i][:], IDS[:, bass.ds(m, 1)]).then_inc(ix_done, 1)
                pool.wait_ge(slots_done, 1)
                pool.wait_ge(ix_done, ready)
                pool.wait_ge(ys_done, done)
                pool.indirect_dma_start(y_d, bass.IndirectOffsetOnAxis(IXS[i][:].bitcast(U32), 0), YS[i][:], None) \
                    .then_inc(y_out[i], 16)

            for m in range(UN - 1):
                gather(m, m, m)

            def slot(m, i, first, last):
                ahead = UN - 1
                if not last or m + ahead < MT:
                    gather(m + ahead, (i + ahead) % UN, 2 * m + ahead)
                    scatter(m, i, 2 * m + ahead + 1)
                else:
                    scatter(m, i, MT + m)

            over_slots(pool, slot)

        @block.scalar
        def _(act):
            act.dma_start(WkS[:], WkT.rearrange("(k p) d -> p k d", p=P)).then_inc(att_in, 16)
            for w, (wT, st) in enumerate(((w1T, stage0), (w2T, stage1))):
                for c in range(KD):
                    act.dma_start(st[:, c, :], wT[P * c:P * c + P, :]).then_inc(w_in[w][c], 16)
            act.dma_start(WoS[:], WoT.rearrange("(k p) d -> p k d", p=P)).then_inc(wo_in, 16)

            def weight_abs(w):
                st = stage1 if w == 1 else stage0
                for c in range(4):
                    act.wait_ge(w_in[w][c], 16)
                    if w or c:
                        act.wait_ge(w_abs, 4 * w + c)
                    nc.scalar.activation(PS[:, 0:4, :].rearrange("p a c -> p (a c)"), st[:, c, :], ACT.Abs,
                                         accum_out=WPART[:, 4 * w + c:4 * w + c + 1]).then_inc(w_abs, 1)

            weight_abs(0)
            weight_abs(1)
            act.wait_ge(repr_T, 1)
            nc.scalar.copy(RT[:].rearrange("p k m -> p (k m)"), bank[7]).then_inc(repr_Tev, 1)
            act.wait_ge(keys_done, 1)
            nc.scalar.activation(KJ[:], bank[5], ACT.Square, accum_out=KSS).then_inc(kss_done, 1)
            act.wait_ge(soft_v, 2)
            nc.scalar.activation(EROW[:, P:2 * P], EROW[:, 0:P], ACT.Exp).then_inc(soft_e, 1)
            act.wait_ge(att_pe, 1)
            nc.scalar.copy(ATT[:], bank[7][:, 256:256 + KD * B]).then_inc(att_copy, 1)
            act.wait_ge(proj_pe, 1)
            nc.scalar.copy(PROJ[0:B, :], bank[4][0:B, :]).then_inc(proj_ev, 1)
            weight_abs(2)

            def square_y(n, t):
                act.wait_ge(y_done, n + 1)
                if not early(n):
                    act.wait_ge(yq_done, n - 1)
                    act.wait_ge(hsq_done, n - 1)
                nc.scalar.activation(JUNK[:, 0:D], Y[t][:], ACT.Square, accum_out=YMS[t]).then_inc(ysq_done, 1)

            def evac_tr1(n, t):
                act.wait_ge(tr1_done, n + 1)
                nc.scalar.copy(QyT[t][:].rearrange("p k m -> p (k m)"), TY[:, 0:D]).then_inc(qyt_done, 1)

            def silu(n, t, c):
                p = NC * n + c
                act.wait_ge(g_done, p + 1)
                if c == 0:
                    act.wait_ge(pool_a, 7 * (n + 1))
                if not (isinstance(n, int) and n == 0 and c < 2):
                    act.wait_ge(hm_done, p - 1)
                nc.scalar.activation(SG[c % 2][:], GP[c % 2], ACT.Silu, scale=OG[t]).then_inc(silu_done, 1)

            def evac_tr2(n):
                for h in range(2):
                    act.wait_ge(tr2_done, 2 * n + h + 1)
                    k = KF // 2
                    nc.scalar.copy(QT[:, k * h:k * h + k, :].rearrange("p k m -> p (k m)"), TR[h]).then_inc(qt_done, 1)

            def square_h(n, t):
                act.wait_ge(hm_done, NC * (n + 1))
                act.wait_ge(ysq_done, n + 2 if not (isinstance(n, int) and n == NT - 1) else NT)
                nc.scalar.activation(JUNK[:], H[t][:], ACT.Square, accum_out=HMS[t]).then_inc(hsq_done, 1)

            square_y(0, 0)
            evac_tr1(0, 0)

            def slot(n, t, first, last):
                silu(n, t, 0)
                silu(n, t, 1)
                if not first:
                    evac_tr2(n - 1)
                silu(n, t, 2)
                silu(n, t, 3)
                if not last:
                    square_y(n + 1, 1 - t)
                square_h(n, t)
                if not last:
                    evac_tr1(n + 1, 1 - t)

            over_tiles(act, slot)
            evac_tr2(NT - 1)

            with act.Fori(0, NG // 2) as gg:
                for h in range(2):
                    for m in range(GI // 4):
                        act.wait_ge(conv_done, (2 * gg + h) * (GI // 4) + m + 1)
                        bk = bank[(h * (GI // 4) + m)]
                        nc.scalar.copy(XP[:, :, bass.ds((2 * gg + h) * GI + 4 * m, 4)],
                                       bk.rearrange("p (i a) -> p a i", i=4)).then_inc(z_done, 1)
            act.wait_ge(z_done, 4 * NG)

            def z_copy(n, t):
                if not early(n):
                    act.wait_ge(zt_pe, n - 1)
                nc.scalar.copy(ZC[t][:].rearrange("p q c -> p (q c)"),
                               XP[:, bass.ds(n * NQ, NQ), :].rearrange("p q c -> p (q c)")).then_inc(zc_done, 1)

            for t in range(TB):
                act.wait_ge(x1_out[t], 16 * B)
            z_copy(0, 0)
            z_copy(1, 1)
            with act.Fori(1, B) as b:
                z_copy(b * TB, 0)
                z_copy(b * TB + 1, 1)
            act.wait_ge(route_v, 15)
            nc.scalar.activation(EX[:], M2[:], ACT.Exp).then_inc(route_e, 1)
            for e in range(E):
                act.wait_ge(we_in[e % (E // 2)], 16 * (2 * e // E + 1))
                if e == 4:
                    act.wait_ge(z_out, 16 * NQ * B)
                nc.scalar.copy(W2[:, where(e), 0], WRAW[e][:]).then_inc(wh_done, 1)

            def slot(m, i, first, last):
                t = i % 2
                act.wait_ge(trz_done, m + 1)
                if not (first and m < 2):
                    act.wait_ge(exp_done, m - 1)
                nc.scalar.copy(ZH[t][:].rearrange("p k m -> p (k m)"), bank[4 + t]).then_inc(zh_done, 1)

            over_slots(act, slot)
            for g in range(NGR):
                act.wait_ge(mix_done, UN * (g + 1))
                dst = out.rearrange("b s d -> (b s) d")[UN * P * g:UN * P * g + UN * P, :].rearrange("(u p) d -> p u d", p=P)
                act.dma_start(dst, X1C[:, UN * g:UN * g + UN, :]).then_inc(out_done, 16)
            act.wait_ge(out_done, 16 * NGR)

        @block.vector
        def _(dve):
            dve.wait_ge(att_in, 48)
            nc.vector.tensor_tensor(RW[:], RW[:], QB[:], ALU.mult).then_inc(rwq_done, 1)

            def ternary(w):
                dve.wait_ge(w_tot, w + 1)
                if w == 2:
                    dve.wait_ge(ysq_done, 1)
                nc.vector.tensor_reduce(WSUM[w], bank[6][:, 4 * w:4 * w + 4], AX.X, ALU.add).then_inc(w_step, 1)
                dve.wait_ge(w_step, 3 * w + 1)
                nc.vector.tensor_scalar(WMEAN[w], WSUM[w], 1.0 / WCOUNT, CLIP, ALU.mult, ALU.max).then_inc(w_step, 1)
                dve.wait_ge(w_step, 3 * w + 2)
                nc.vector.reciprocal(WSC[w], WMEAN[w]).then_inc(w_step, 1)
                dve.wait_ge(w_step, 3 * w + 3)
                st = stage1 if w == 1 else stage0
                for c in range(4):
                    if w == 2:
                        dst = W3[:].rearrange("p k d -> p (k d)")[:, FF * c:FF * c + FF]
                    else:
                        dst = W12[:, c, FF * w:FF * w + FF]
                    if w or c:
                        dve.wait_ge(w_tern, 4 * w + c)
                    nc.vector.tensor_scalar(TMP[:], st[:, c, :], WSC[w], 1.0, ALU.mult, ALU.min).then_inc(w_round, 1)
                    dve.wait_ge(w_round, 4 * w + c + 1)
                    nc.vector.tensor_scalar(dst, TMP[:], -1.0, None, ALU.max).then_inc(w_tern, 1)

            ternary(0)
            dve.wait_ge(repr_sum, 1)
            nc.vector.tensor_copy(R[:], bank[5]).then_inc(repr_ev, 1)
            dve.wait_ge(keys_done, 1)
            dve.wait_ge(kss_done, 1)
            dve.wait_ge(rwq_done, 1)
            nc.vector.tensor_tensor_reduce(QB[:], bank[5], RW[:], 1.0, 0.0, ALU.mult, ALU.add, DOT).then_inc(dot_done, 1)
            dve.wait_ge(dot_done, 1)
            dve.wait_ge(krs_done, 1)
            nc.vector.tensor_tensor(SCO, DOT, KRS, ALU.mult).then_inc(sco_done, 1)
            dve.wait_ge(row_done, 1)
            row = bank[7][0:1, 0:P].rearrange("o (b k) -> o b k", k=BLK)
            nc.vector.tensor_reduce(GMX, row, AX.X, ALU.max).then_inc(soft_v, 1)
            dve.wait_ge(soft_v, 1)
            er = EROW[:, 0:P].rearrange("o (b k) -> o b k", k=BLK)
            ee = EROW[:, P:2 * P].rearrange("o (b k) -> o b k", k=BLK)
            nc.vector.tensor_tensor(er, row, GMX.rearrange("o (b k) -> o b k", k=1).broadcast_to([1, B, BLK]),
                                    ALU.subtract).then_inc(soft_v, 1)
            dve.wait_ge(soft_e, 1)
            nc.vector.tensor_reduce(GSM, ee, AX.X, ALU.add).then_inc(soft_v, 1)
            dve.wait_ge(soft_v, 3)
            nc.vector.reciprocal(GMX, GSM).then_inc(soft_v, 1)
            dve.wait_ge(soft_v, 4)
            nc.vector.tensor_tensor(ROWS[:].rearrange("o (b k) -> o b k", k=BLK), ee,
                                    GMX.rearrange("o (b k) -> o b k", k=1).broadcast_to([1, B, BLK]),
                                    ALU.mult).then_inc(soft_v, 1)
            dve.wait_ge(colT_done, 1)
            nc.vector.tensor_copy(ATC, bank[7][:, P:P + 1]).then_inc(att_v, 1)
            dve.wait_ge(att_v, 1)
            dve.wait_ge(const, 8)
            nc.vector.tensor_scalar(AMX[:], MSK[:], ATC, None, ALU.mult).then_inc(att_v, 1)
            ternary(1)

            def front_1(n, t):
                dve.wait_ge(pj_in[t], 16 * (n // 2 + 1) if isinstance(n, int) else 8 * (n - t) + 16)
                nc.vector.tensor_tensor(SUM[t][:], X[:, n, :] if isinstance(n, int) else X[:, bass.ds(n, 1), :].rearrange("p o d -> p (o d)"),
                                        PJ[t][:], ALU.add).then_inc(sum_done, 1)
                dve.wait_ge(sum_done, n + 1)
                nc.vector.bn_stats(BS[t], SUM[t][:]).then_inc(stats_done, 1)

            def front_2(n, t):
                dve.wait_ge(norm_in, 32)
                dve.wait_ge(stats_done, n + 1)
                nc.vector.bn_aggr(MV[t], BS[t]).then_inc(mv_done, 1)
                dve.wait_ge(mv_done, n + 1)
                nc.vector.scalar_tensor_tensor(out=SUM[t][:], in0=SUM[t][:], scalar=MV[t][:, 0:1], in1=GAM[:],
                                               op0=ALU.subtract, op1=ALU.mult).then_inc(gam_done, 1)

            def front_3(n, t):
                dve.wait_ge(gam_done, n + 1)
                dve.wait_ge(rstd_done, n + 1)
                if not early(n):
                    dve.wait_ge(ysq_done, n - 1)
                nc.vector.scalar_tensor_tensor(out=Y[t][:], in0=SUM[t][:], scalar=RSTD[t], in1=BET[:],
                                               op0=ALU.mult, op1=ALU.add).then_inc(y_done, 1)
                dve.wait_ge(y_done, n + 1)
                nc.vector.tensor_reduce(YM[t], Y[t][:], AX.X, ALU.max, apply_absolute_value=True).then_inc(ymax_done, 1)

            def front_4(n, t):
                dve.wait_ge(yo_done, n + 1)
                nc.vector.reciprocal(YI[t], YO[t]).then_inc(yi_done, 1)

            def front_5(n, t):
                dve.wait_ge(yq_done, n + 1)
                nc.vector.tensor_scalar(Iy[:], Y[t][:], YQ[t], QMAX, ALU.mult, ALU.min).then_inc(yint_done, 1)
                dve.wait_ge(yint_done, n + 1)
                if not early(n):
                    dve.wait_ge(tr1_done, n - 1)
                nc.vector.tensor_copy(Qy[t][:], Iy[:]).then_inc(yqt_done, 1)

            def h_mul(n, t, c):
                p = NC * n + c
                dve.wait_ge(u_done, p + 1)
                dve.wait_ge(silu_done, p + 1)
                if not early(n) and c == 0:
                    dve.wait_ge(hsq_done, n - 1)
                nc.vector.tensor_tensor(H[t][:, CH * c:CH * c + CH], SG[c % 2][:], UP[c % 2], ALU.mult).then_inc(hm_done, 1)

            def h_max(n, t):
                dve.wait_ge(hm_done, NC * (n + 1))
                nc.vector.tensor_reduce(HM[t], H[t][:], AX.X, ALU.max, apply_absolute_value=True).then_inc(hmax_done, 1)

            def h_quant(n, t):
                dve.wait_ge(ho_done, n + 1)
                nc.vector.reciprocal(HI[t], HO[t]).then_inc(hi_done, 1)
                dve.wait_ge(hq_done, n + 1)
                nc.vector.tensor_scalar(Ih[:], H[t][:], HQ[t], QMAX, ALU.mult, ALU.min).then_inc(hint_done, 1)
                dve.wait_ge(hint_done, n + 1)
                if not (isinstance(n, int) and n == 0):
                    dve.wait_ge(tr2_done, 2 * n)
                nc.vector.tensor_copy(Qh[:], Ih[:]).then_inc(qh_done, 1)

            def x1_add(n, t):
                dve.wait_ge(down_done, n + 1)
                if not early(n):
                    dve.wait_ge(x1_out[t], 16 * ((n - t) // 2) if isinstance(n, int) else 8 * (n - t))
                dve.wait_ge(pool_h, 7 * (n + 1))
                xn = X[:, n, :] if isinstance(n, int) else X[:, bass.ds(n, 1), :].rearrange("p o d -> p (o d)")
                nc.vector.scalar_tensor_tensor(out=X1[t][:], in0=DN, scalar=OD[t], in1=xn,
                                               op0=ALU.mult, op1=ALU.add).then_inc(x1_done, 1)

            dve.wait_ge(norm_in, 32)
            front_1(0, 0)
            front_2(0, 0)
            front_3(0, 0)
            front_4(0, 0)
            front_5(0, 0)
            ternary(2)

            def slot(n, t, first, last):
                h_mul(n, t, 0)
                if not last:
                    front_1(n + 1, 1 - t)
                h_mul(n, t, 1)
                if not last:
                    front_2(n + 1, 1 - t)
                h_mul(n, t, 2)
                if not last:
                    front_3(n + 1, 1 - t)
                h_mul(n, t, 3)
                if not last:
                    front_4(n + 1, 1 - t)
                h_max(n, t)
                if not last:
                    front_5(n + 1, 1 - t)
                h_quant(n, t)
                if not first:
                    x1_add(n - 1, 1 - t)

            over_tiles(dve, slot)
            x1_add(NT - 1, 1)

            nc.vector.memset(BD[0][:], 0.0).then_inc(bd_zero, 1)
            dve.wait_ge(bd_zero, 2)
            dve.wait_ge(T_in, 16 * NQ)

            def spread(g, h, first):
                if not first:
                    dve.wait_ge(conv_done, (g - 1) * (GI // 4))
                for j in range(NQ):
                    q = slice(QD * j, QD * j + QD)
                    i = nc.vector.tensor_copy(BD[h][q, :, :, q][:, :, :, ::-1],
                                             
                                              T[q, bass.ds(g * GI, GI), :].rearrange("p i (w u) -> p w i u", w=2))
                i.then_inc(bd_done, 1)

            spread(0, 0, True)
            spread(1, 1, True)
            with dve.Fori(1, NG // 2) as gg:
                spread(2 * gg, 0, False)
                spread(2 * gg + 1, 1, False)

            for t in range(TB):
                dve.wait_ge(x1_out[t], 16 * B)

            def z_turned(n, t):
                dve.wait_ge(zt_pe, n + 1)
                if not early(n):
                    dve.wait_ge(lg_done, n - 1)
                nc.vector.tensor_copy(ZT[t][:].rearrange("p j (q u) -> p q j u", q=NQ),
                                      bank[4 + t].rearrange("p (q j u) -> p q j u", q=NQ, j=NQ)).then_inc(zt_done, 1)

            z_turned(0, 0)
            z_turned(1, 1)
            with dve.Fori(1, B) as b:
                z_turned(b * TB, 0)
                z_turned(b * TB + 1, 1)

            def wide(m):
                return m[:].rearrange("p (n o) -> p n o", o=1).broadcast_to([P, NT, E])

            step = [0]

            def v(i):
                step[0] += 1
                i.then_inc(route_v, 1)
                dve.wait_ge(route_v, step[0])

            dve.wait_ge(lg_done, NT)
            dve.wait_ge(route_p, 1)
            v(nc.vector.tensor_copy(CAND[:], IOE[:].bitcast(I32)))
            v(nc.vector.tensor_scalar(IOE[:], CAND[:], -float(E), None, ALU.add))
            v(nc.vector.tensor_copy(LG[:].rearrange("p n e -> p (n e)"), bank[6][:, 0:NR]))
            v(nc.vector.tensor_reduce(M1[:], LG[:], AX.X, ALU.max))
            v(nc.vector.tensor_tensor(OH1[:], LG[:], wide(M1), ALU.is_equal))
            v(nc.vector.tensor_tensor(CAND[:], OH1[:], IOE[:], ALU.mult))
            v(nc.vector.tensor_reduce(S1[:], CAND[:], AX.X, ALU.min))
            v(nc.vector.tensor_tensor(OH1[:], IOE[:], wide(S1), ALU.is_equal))
            v(nc.vector.scalar_tensor_tensor(out=L2[:], in0=OH1[:], scalar=-3e38, in1=LG[:], op0=ALU.mult, op1=ALU.add))
            v(nc.vector.tensor_reduce(M2[:], L2[:], AX.X, ALU.max))
            v(nc.vector.tensor_tensor(OH2[:], L2[:], wide(M2), ALU.is_equal))
            v(nc.vector.tensor_tensor(CAND[:], OH2[:], IOE[:], ALU.mult))
            v(nc.vector.tensor_reduce(S2[:], CAND[:], AX.X, ALU.min))
            v(nc.vector.tensor_tensor(OH2[:], IOE[:], wide(S2), ALU.is_equal))
            v(nc.vector.tensor_tensor(M2[:], M2[:], M1[:], ALU.subtract))
            nc.vector.tensor_tensor(CNT[:], OH1[:], OH2[:], ALU.add).then_inc(cnt_done, 1)
            dve.wait_ge(route_p, 6)
            v(nc.vector.tensor_copy(IOSF[:], IOS[:]))
            v(nc.vector.tensor_copy(IOSB[:], IOSF[:]))
            v(nc.vector.tensor_copy(PIDX[:], PIDI[:]))
            v(nc.vector.tensor_copy(PADF[:], PADI[:]))
            dve.wait_ge(route_e, 1)
            v(nc.vector.tensor_scalar(P1[:], EX[:], 1.0, None, ALU.add))
            v(nc.vector.reciprocal(P1[:], P1[:]))
            v(nc.vector.tensor_tensor(P2[:], P1[:], EX[:], ALU.mult))
            dve.wait_ge(pre_done, 2)
            PRE, TOT = (bank[i][:, 0:NR].rearrange("p (n e) -> p n e", e=E) for i in (4, 5))
            v(nc.vector.tensor_copy(SA[:], TOT))
            src, dst, d = SA, SB, 1
            while d < NT:
                nc.vector.tensor_copy(dst[:, 0:d, :], src[:, 0:d, :])
                v(nc.vector.tensor_tensor(dst[:, d:NT, :], src[:, d:NT, :], src[:, 0:NT - d, :], ALU.add))
                src, dst, d = dst, src, 2 * d
            upto = src
            v(nc.vector.tensor_scalar(TEI[:], upto[:, NT - 1, :], 1.0 / P, 0.5 - 0.5 / P, ALU.mult, ALU.add))
            v(nc.vector.tensor_copy(TE[:], TEI[:]))
            v(nc.vector.tensor_copy(ENDA[:], TEI[:]))
            src, dst, d = ENDA, ENDB, 1
            while d < E:
                nc.vector.tensor_copy(dst[:, 0:d], src[:, 0:d])
                v(nc.vector.tensor_tensor(dst[:, d:E], src[:, d:E], src[:, 0:E - d], ALU.add))
                src, dst, d = dst, src, 2 * d
            END = src
            v(nc.vector.tensor_tensor(STA[:], END[:], TE[:], ALU.subtract))
            v(nc.vector.tensor_tensor(upto[:], upto[:], TOT, ALU.subtract))
            v(nc.vector.tensor_tensor(upto[:], upto[:], PRE, ALU.add))
            v(nc.vector.scalar_tensor_tensor(out=upto[:], in0=STA[:].rearrange("p (o e) -> p o e", o=1).broadcast_to([P, NT, E]),
                                             scalar=float(P), in1=upto[:], op0=ALU.mult, op1=ALU.add))
            for k, oh in enumerate((OH1, OH2)):
                v(nc.vector.tensor_tensor(CAND[:], oh[:], upto[:], ALU.mult))
                v(nc.vector.tensor_reduce(POS[:, NT * k:NT * k + NT], CAND[:], AX.X, ALU.add))
            v(nc.vector.tensor_scalar(MTI[:], POS[:], 1.0 / P, 0.5 / P - 0.5, ALU.mult, ALU.add))
            v(nc.vector.tensor_copy(MTF[:], MTI[:]))
            nc.vector.tensor_copy(MTB[:], MTI[:])
            v(nc.vector.scalar_tensor_tensor(out=SLB[:], in0=MTF[:], scalar=-float(P), in1=POS[:], op0=ALU.mult, op1=ALU.add))
            for q in range(NK // CC):
                h = q % 2
                cols = slice(CC * q, CC * q + CC)
                if q >= 2:
                    dve.wait_ge(tab_done, q - 1)

                def along(t, n):
                    return t[:, cols].rearrange("p (c o) -> p c o", o=1).broadcast_to([P, CC, n])

                def over(t, first, n):
                    return t[:, first:first + n].rearrange("p (o n) -> p o n", o=1).broadcast_to([P, CC, n])

                v(nc.vector.tensor_tensor(BOH[h][:, :, 0, :], over(IOSB, 0, MT), along(MTB, MT), ALU.is_equal))
                nc.vector.tensor_tensor(AOH[h][:], over(IOSB, 0, P), along(SLB, P), ALU.is_equal).then_inc(oh_done, 1)
                v(nc.vector.tensor_scalar(BOH[h][:, :, 1, :], BOH[h][:, :, 0, :], PIDX[:, 0:1], None, ALU.mult))
                number = IOSB[:, CC * q + 1:CC * q + CC + 1].rearrange("p (c o) -> p c o", o=1).broadcast_to([P, CC, MT])
                nc.vector.tensor_tensor(BOH[h][:, :, 0, :], BOH[h][:, :, 0, :], number, ALU.mult).then_inc(oh_done, 1)
            v(nc.vector.tensor_tensor(GE[:], IOSF[0:1, 0:MT].rearrange("p (m o) -> p m o", o=1).broadcast_to([1, MT, E]),
                                      END[0:1, :].rearrange("p (o e) -> p o e", o=1).broadcast_to([1, MT, E]), ALU.is_ge))
            v(nc.vector.tensor_reduce(TEF[:], GE[:], AX.X, ALU.add))
            v(nc.vector.tensor_scalar(TEF[:], TEF[:], float(E - 1), None, ALU.min))
            v(nc.vector.tensor_copy(TEXP[:], TEF[:]))
            v(nc.vector.tensor_scalar(TEK[:], TEF[:], E / 2 - 0.5, -float(E), ALU.is_ge, ALU.mult))
            v(nc.vector.scalar_tensor_tensor(out=TPLC[:], in0=TEF[:], scalar=E / 2, in1=TEK[:], op0=ALU.add, op1=ALU.add))
            dve.wait_ge(tab_done, NK // CC)
            NUM, PART = bank[7][:, 0:MT], bank[7][:, MT:2 * MT]
            v(nc.vector.tensor_copy(TSUM[:], PART))
            v(nc.vector.scalar_tensor_tensor(out=TSUM[:], in0=NUM, scalar=float(P), in1=TSUM[:], op0=ALU.mult, op1=ALU.add))
            v(nc.vector.scalar_tensor_tensor(out=TPAD[:], in0=NUM, scalar=0.5, in1=PADF[:], op0=ALU.is_lt, op1=ALU.mult))
            v(nc.vector.scalar_tensor_tensor(out=IDS[:], in0=TSUM[:], scalar=-float(P), in1=TPAD[:], op0=ALU.add, op1=ALU.add))
            v(nc.vector.tensor_scalar(TTOK[:], NUM, NT + 0.5, -float(TOK), ALU.is_ge, ALU.mult))
            v(nc.vector.tensor_tensor(TTOK[:], TTOK[:], TSUM[:], ALU.add))
            nc.vector.tensor_scalar(IDG[:], TTOK[:], -float(P), 0.0, ALU.add, ALU.max).then_inc(slots_done, 1)
            for e in range(EP, E):
                dve.wait_ge(wh_done, e + 1)
                nc.vector.tensor_tensor(W2[:, where(e), 1], WRAW[e][:], W2[:, where(e), 0].bitcast(F32), ALU.subtract).then_inc(wl_dve, 1)

            def z_low(m, t, early):
                dve.wait_ge(zh_done, m + 1)
                if not early:
                    dve.wait_ge(exp_done, m - 1)
                nc.vector.tensor_tensor(ZL[t][:].rearrange("p k m -> p (k m)"), bank[4 + t],
                                        ZH[t][:].rearrange("p k m -> p (k m)").bitcast(F32), ALU.subtract).then_inc(zl_done, 1)

            dve.wait_ge(be_in, 16)
            z_low(0, 0, True)

            def slot(m, i, first, last):
                if not last or m + 1 < MT:
                    z_low(m + 1, (i + 1) % 2, first and m + 1 < 2)
                e = dve.value_load(TEXP[0:1, bass.ds(m, 1)], min_val=0, max_val=E - 1)
                dve.wait_ge(exp_done, m + 1)
                if not first:
                    dve.wait_ge(y_out[i], 16 * (m // UN) if isinstance(m, int) else 4 * (m - i))
                nc.vector.tensor_tensor(YS[i][:], bank[i], BEB[:, bass.ds(e, 1), :].rearrange("p o d -> p (o d)"),
                                        ALU.add).then_inc(ys_done, 1)

            over_slots(dve, slot)
            for g in range(NGR):
                yc = YC[g % (NGR // 2)]
                half = g // (NGR // 2)
                dve.wait_ge(x1c_in[g % (NGR // 2)], 16 * (half + 1))
                dve.wait_ge(yc_in[g % (NGR // 2)], 32 * (half + 1))
                for u in range(UN):
                    n = UN * g + u
                    nc.vector.scalar_tensor_tensor(out=X1C[:, n, :], in0=yc[0][:, u, :], scalar=P1[:, n:n + 1], in1=X1C[:, n, :],
                                                   op0=ALU.mult, op1=ALU.add).then_inc(mix_a, 1)
                for u in range(UN):
                    n = UN * g + u
                    dve.wait_ge(mix_a, n + 1)
                    nc.vector.scalar_tensor_tensor(out=X1C[:, n, :], in0=yc[1][:, u, :], scalar=P2[:, n:n + 1], in1=X1C[:, n, :],
                                                   op0=ALU.mult, op1=ALU.add).then_inc(mix_done, 1)

        @block.tensor
        def _(pe):
            pe.wait_ge(const, 8)
            for n in range(NT):
                if n % (NT // 8) == 0:
                    pe.wait_ge(x_in[n // (NT // 8)], 16)
                o = P - NQ - NQ * n
                i = nc.tensor.matmul(bank[5], SELW[:, o:o + P], X[:, n, :], start=(n == 0), stop=(n == NT - 1))
            i.then_inc(repr_sum, 1)

            def weight_total(w):
                pe.wait_ge(w_abs, 4 * w + 4)
                if w:
                    pe.wait_ge(w_step, 3 * w - 2)
                nc.tensor.matmul(bank[6][:, 4 * w:4 * w + 4], ONES[:], WPART[:, 4 * w:4 * w + 4],
                                 start=True, stop=True).then_inc(w_tot, 1)

            weight_total(0)
            pe.wait_ge(repr_ev, 1)
            for k in range(KD):
                i = nc.tensor.transpose(bank[7][:, P * k:P * k + P], R[:, P * k:P * k + P], IDF[:])
            i.then_inc(repr_T, 1)
            pe.wait_ge(repr_Tev, 1)
            pe.wait_ge(att_in, 48)
            for k in range(KD):
                i = nc.tensor.matmul(bank[5], RT[:, k, :], WkS[:, k, :], start=(k == 0), stop=(k == KD - 1))
            i.then_inc(keys_done, 1)
            pe.wait_ge(sco_done, 1)
            nc.tensor.matmul(bank[7][0:1, 0:P], SCO, IDF[:], start=True, stop=True).then_inc(row_done, 1)
            pe.wait_ge(soft_v, 5)
            nc.tensor.matmul(bank[7][:, P:P + 1], ROWS[:], ONES[0:1, 0:1], start=True, stop=True).then_inc(colT_done, 1)
            pe.wait_ge(att_v, 2)
            for k in range(KD):
                i = nc.tensor.matmul(bank[7][:, 256 + B * k:256 + B * k + B], R[:, P * k:P * k + P], AMX[:],
                                     start=True, stop=True)
            i.then_inc(att_pe, 1)
            pe.wait_ge(att_copy, 1)
            pe.wait_ge(wo_in, 16)
            for k in range(KD):
                i = nc.tensor.matmul(bank[4][0:B, :], ATT[:, B * k:B * k + B], WoS[:, k, :],
                                     start=(k == 0), stop=(k == KD - 1))
            i.then_inc(proj_pe, 1)
            weight_total(1)
            weight_total(2)

            def turn_y(n, t):
                pe.wait_ge(yqt_done, n + 1)
                if not (isinstance(n, int) and n == 0):
                    pe.wait_ge(qyt_done, n)
                for k in range(KD):
                    i = nc.tensor.transpose(TY[:, P * k:P * k + P], Qy[t][:, P * k:P * k + P], IDB[:])
                i.then_inc(tr1_done, 1)

            def up(n, t, c):
                p = NC * n + c
                if c == 0:
                    pe.wait_ge(qyt_done, n + 1)
                free = not (isinstance(n, int) and n == 0 and c < 2)
                if free:
                    pe.wait_ge(silu_done, p - 1)
                for k in range(KD):
                    i = nc.tensor.matmul(GP[c % 2], QyT[t][:, k, :], W12[:, k, CH * c:CH * c + CH],
                                         start=(k == 0), stop=(k == KD - 1))
                i.then_inc(g_done, 1)
                if free:
                    pe.wait_ge(hm_done, p - 1)
                for k in range(KD):
                    i = nc.tensor.matmul(UP[c % 2], QyT[t][:, k, :], W12[:, k, FF + CH * c:FF + CH * c + CH],
                                         start=(k == 0), stop=(k == KD - 1))
                i.then_inc(u_done, 1)

            def turn_h(n):
                pe.wait_ge(qh_done, n + 1)
                for h in range(2):
                    if not (isinstance(n, int) and n == 0):
                        pe.wait_ge(qt_done, 2 * n + h - 1)
                    for k in range(KF // 2):
                        kk = KF // 2 * h + k
                        i = nc.tensor.transpose(TR[h][:, P * k:P * k + P], Qh[:, P * kk:P * kk + P], IDB[:])
                    i.then_inc(tr2_done, 1)

            def down(n):
                if not (isinstance(n, int) and n == 0):
                    pe.wait_ge(x1_done, n)
                for k in range(KF):
                    if k % (KF // 2) == 0:
                        pe.wait_ge(qt_done, 2 * n + k // (KF // 2) + 1)
                    i = nc.tensor.matmul(DN, QT[:, k, :], W3[:, k, :], start=(k == 0), stop=(k == KF - 1))
                i.then_inc(down_done, 1)

            turn_y(0, 0)
            pe.wait_ge(w_tern, 12)

            def slot(n, t, first, last):
                up(n, t, 0)
                up(n, t, 1)
                if not first:
                    turn_h(n - 1)
                up(n, t, 2)
                up(n, t, 3)
                if not first:
                    down(n - 1)
                if not last:
                    turn_y(n + 1, 1 - t)

            over_tiles(pe, slot)
            turn_h(NT - 1)
            down(NT - 1)

            pe.wait_ge(xp_in, 16 * NQ * B)
            pe.wait_ge(x1_done, NT)

            def conv(g, h, first):
                pe.wait_ge(bd_done, g + 1)
                for i in range(GI):
                    m = i // 4
                    if i % 4 == 0 and not first:
                        pe.wait_ge(z_done, (g - 2) * (GI // 4) + m + 1)
                    o = bank[h * (GI // 4) + m][:, NBLK * (i % 4):NBLK * (i % 4) + NBLK]
                    xi = XP[:, :, bass.ds(g * GI + i, 1)].rearrange("p a o -> p (a o)")
                    nc.tensor.matmul(o, BD[h][:, 1, i, :], xi, start=True, stop=False)
                    mm = nc.tensor.matmul(o.rearrange("p (b k) -> p b k", k=BLK)[:, :, 1:BLK], BD[h][:, 0, i, :],
                                          xi.rearrange("p (b k) -> p b k", k=BLK)[:, :, 0:BLK - 1],
                                          start=False, stop=True)
                    if i % 4 == 3:
                        mm.then_inc(conv_done, 1)

            conv(0, 0, True)
            conv(1, 1, True)
            with pe.Fori(1, NG // 2) as gg:
                conv(2 * gg, 0, False)
                conv(2 * gg + 1, 1, False)

            pe.wait_ge(z_done, 4 * NG)
            pe.wait_ge(route_in, 16)

            def turn_z(n, t):
                pe.wait_ge(zc_done, n + 1)
                if not early(n):
                    pe.wait_ge(zt_done, n - 1)
                for q in range(NQ):
                    i = nc.tensor.transpose(bank[4 + t][:, P * q:P * q + P], ZC[t][:, q, :], IDF[:])
                i.then_inc(zt_pe, 1)

            def logits(n, t):
                pe.wait_ge(zt_done, n + 1)
                for j in range(NQ):
                    i = nc.tensor.matmul(bank[6][:, bass.ds(n * E, E)], ZT[t][:, j, :], WRS[:, j, :],
                                         start=(j == 0), stop=(j == NQ - 1))
                i.then_inc(lg_done, 1)

            turn_z(0, 0)
            turn_z(1, 1)
            logits(0, 0)
            turn_z(2, 0)
            logits(1, 1)
            with pe.Fori(1, B - 1) as b:
                for t in range(TB):
                    turn_z(b * TB + t + 1, 1 - t)
                    logits(b * TB + t, t)
            turn_z(NT - 1, 1)
            logits(NT - 2, 0)
            logits(NT - 1, 1)

            pe.wait_ge(cnt_done, 1)
            pe.wait_ge(route_p, 6)
            cnt = CNT[:].rearrange("p n e -> p (n e)")
            nc.tensor.matmul(bank[4][:, 0:NR], TRI[:], cnt, start=True, stop=True).then_inc(pre_done, 1)
            nc.tensor.matmul(bank[5][:, 0:NR], ONB[:], cnt, start=True, stop=True).then_inc(pre_done, 1)
            for q in range(NK // CC):
                pe.wait_ge(oh_done, 2 * q + 2)
                for c in range(CC):
                    i = nc.tensor.matmul(bank[7][:, 0:2 * MT], AOH[q % 2][:, c, :], BOH[q % 2][:, c, :, :].rearrange("p v m -> p (v m)"),
                                         start=(q == 0 and c == 0), stop=(q == NK // CC - 1 and c == CC - 1))
                i.then_inc(tab_done, 1)

            def turn_r(m, i, early):
                t = i % 2
                pe.wait_ge(zr_in[i], 16 * (m // UN + 1) if isinstance(m, int) else 4 * (m - i) + 16)
                if not early:
                    pe.wait_ge(zl_done, m - 1)
                for k in range(KD):
                    x = nc.tensor.transpose(bank[4 + t][:, P * k:P * k + P], ZR[i][:, P * k:P * k + P], IDF[:])
                x.then_inc(trz_done, 1)

            pe.wait_ge(slots_done, 1)
            turn_r(0, 0, True)
            pe.wait_ge(wl_pool, EP)
            pe.wait_ge(wl_dve, E - EP)

            def slot(m, i, first, last):
                if not last or m + 1 < MT:
                    turn_r(m + 1, (i + 1) % UN, first and m + 1 < 2)
                q = pe.value_load(TPLC[0:1, bass.ds(m, 1)], min_val=0, max_val=E - 1)
                pe.wait_ge(zl_done, m + 1)
                if not first:
                    pe.wait_ge(ys_done, m - UN + 1)
                for k in range(KD):
                    for n, (zz, part) in enumerate(((ZH, 0), (ZH, 1), (ZL, 0))):
                        x = nc.tensor.matmul(bank[i], zz[i % 2][:, k, :], W2[:, bass.ds(q, 1), part, k, :].rearrange("p o d -> p (o d)"),
                                             start=(k == 0 and n == 0), stop=(k == KD - 1 and n == 2))
                x.then_inc(exp_done, 1)

            over_slots(pe, slot)


def kernel(**inputs):
    import numpy as np
    import concourse.bacc as bacc
    from concourse.bass_utils import run_bass_kernel_spmd

    arrays = {
        "x": inputs["x"],
        "cond": inputs["cond_2048"],
        "taps": np.asarray(inputs["cond_2048"]).T,
        "rms_w": inputs["L0_cond_rms_weight"],
        "WkT": np.asarray(inputs["L0_cond_Wk"]).T,
        "WoT": np.asarray(inputs["L0_cond_Wo"]).T,
        "gamma": inputs["L0_cond_ln_gamma"],
        "beta": inputs["L0_cond_ln_beta"],
        "w1T": np.asarray(inputs["L0_ffn_w1"]).T,
        "w2T": np.asarray(inputs["L0_ffn_w2"]).T,
        "w3T": np.asarray(inputs["L0_ffn_w3"]).T,
        "Wr": inputs["L1_ffn_Wr"],
        "We": inputs["L1_ffn_We"],
        "be": inputs["L1_ffn_be"],
    }
    nc = bacc.Bacc("TRN2", target_bir_lowering=False, num_devices=1)
    feed, args = {}, []
    for name, a in arrays.items():
        a = np.ascontiguousarray(a)
        feed[f"in_{name}"] = a
        args.append(nc.dram_tensor(f"in_{name}", a.shape, mybir.dt.from_np(a.dtype), kind="ExternalInput").ap())
    out = nc.dram_tensor("out_x", tuple(arrays["x"].shape), F32, kind="ExternalOutput").ap()
    adaln_ffn_moe(nc, *args, out)
    r = run_bass_kernel_spmd(nc, [feed], core_ids=[0])
    return r.results[0]["out_x"]
```
